# Optimizing a Trainium2 kernel written in Bass

```python
import numpy as np
import jax
import jax.numpy as jnp

def _softmax(x, axis=-1):
    return jax.nn.softmax(x, axis=axis)

def _gelu(x):
    return jax.nn.gelu(x, approximate=True)

def _silu(x):
    return jax.nn.silu(x)

def _sigmoid(x):
    return jax.nn.sigmoid(x)

def _layernorm(x, axis=-1, eps=1e-05):
    m = jnp.mean(x, axis=axis, keepdims=True)
    v = jnp.var(x, axis=axis, keepdims=True)
    return (x - m) / jnp.sqrt(v + eps)

def _scatter_add(tgt, idx, src, axis=0):
    return tgt.at[idx].add(src)

def _segment_sum(src, seg, n):
    return jax.ops.segment_sum(src, seg, n)
kernel_name = 'mk_sandwich_d2_jaxref_r8_ad774d'

def setup_inputs(seed: int=0):
    np.random.seed(seed)
    _w = jnp.asarray

    def _L0_attn_setup():
        import math
        import jax, jax.numpy as jnp
        import numpy as np

        def _alibi_slopes(n):

            def pow2_slopes(n):
                start = 2.0 ** (-2.0 ** (-(math.log2(n) - 3)))
                return [start * start ** i for i in range(n)]
            if math.log2(n).is_integer():
                return pow2_slopes(n)
            cp2 = 2 ** math.floor(math.log2(n))
            return pow2_slopes(cp2) + _alibi_slopes(2 * cp2)[0::2][:n - cp2]
        NUM_HEADS = 16
        key = jax.random.key(seed)
        ks = jax.random.split(key, 5)
        B, S, H = (2, 256, 256)
        return {'hidden_states': jax.random.normal(ks[0], (B, S, H), jnp.float32), 'w_qkv': jax.random.normal(ks[1], (H, 3 * H), jnp.float32) * H ** (-0.5), 'b_qkv': jax.random.normal(ks[2], (3 * H,), jnp.float32) * 0.02, 'w_proj': jax.random.normal(ks[3], (H, H), jnp.float32) * H ** (-0.5), 'b_proj': jax.random.normal(ks[4], (H,), jnp.float32) * 0.02}
    _L0_attn_in = _L0_attn_setup()

    def _L0_ffn_setup():
        import jax, jax.numpy as jnp
        import numpy as np
        B, T, D = (2, 128, 256)
        E, F, K = (64, 64, 4)
        S, HS = (2, 64 * 4)
        key = jax.random.key(seed)
        ks = jax.random.split(key, 9)
        s = 0.02
        f32 = jnp.float32
        return {'x': jax.random.normal(ks[0], (B, T, D), f32), 'router_w': jax.random.normal(ks[1], (D, E), f32) * s, 'router_bias': jnp.zeros((E,), f32), 'wg': jax.random.normal(ks[2], (E, D, F), f32) * s, 'wu': jax.random.normal(ks[3], (E, D, F), f32) * s, 'wd': jax.random.normal(ks[4], (E, F, D), f32) * s, 'swg': jax.random.normal(ks[5], (S, D, HS), f32) * s, 'swu': jax.random.normal(ks[6], (S, D, HS), f32) * s, 'swd': jax.random.normal(ks[7], (S, HS, D), f32) * s}
    _L0_ffn_in = _L0_ffn_setup()

    def _L1_attn_setup():
        import jax, jax.numpy as jnp
        import numpy as np
        B, L, DM = (2, 256, 256)
        EXPAND, D_STATE, D_CONV, H, CS = (2, 128, 4, 32, 32)
        D_INNER = EXPAND * DM
        HD = D_INNER // H
        N = D_STATE
        PROJ = 2 * D_INNER + 2 * H * N + H
        key = jax.random.key(seed)
        ks = jax.random.split(key, 8)
        x = jax.random.normal(ks[0], (B, L, DM), jnp.float32)
        W_in = jax.random.normal(ks[1], (PROJ, DM), jnp.float32) * 0.02
        conv_w = jax.random.normal(ks[2], (D_INNER, 1, D_CONV), jnp.float32) * 0.2
        conv_b = jnp.zeros((D_INNER,), jnp.float32)
        A_log = jnp.full((H,), jnp.log(2.0), jnp.float32)
        D_param = jnp.ones((D_INNER,), jnp.float32)
        dt_bias = jnp.zeros((H,), jnp.float32)
        W_out = jax.random.normal(ks[3], (DM, D_INNER), jnp.float32) * 0.02
        return {'x': x, 'W_in': W_in, 'conv_w': conv_w, 'conv_b': conv_b, 'A_log': A_log, 'D_param': D_param, 'dt_bias': dt_bias, 'W_out': W_out}
    _L1_attn_in = _L1_attn_setup()

    def _L1_ffn_setup():
        import jax, jax.numpy as jnp
        import numpy as np
        key = jax.random.key(seed)
        k1, k2, k3, k4, k5 = jax.random.split(key, 5)
        B, L, H, N = (2, 256, 256, 1024)
        x = jax.random.normal(k1, (B, L, H), dtype=jnp.float32)
        W0 = jax.random.normal(k2, (N, H), dtype=jnp.float32) * (1.0 / np.sqrt(H))
        bias0 = jax.random.normal(k3, (N,), dtype=jnp.float32) * 0.02
        W1 = jax.random.normal(k4, (H, N), dtype=jnp.float32) * (1.0 / np.sqrt(N))
        bias1 = jax.random.normal(k5, (H,), dtype=jnp.float32) * 0.02
        return {'x': x, 'W0': W0, 'bias0': bias0, 'W1': W1, 'bias1': bias1}
    _L1_ffn_in = _L1_ffn_setup()
    _d = {'L0_attn_hidden_states': _L0_attn_in['hidden_states'], 'L0_attn_w_qkv': _L0_attn_in['w_qkv'], 'L0_attn_b_qkv': _L0_attn_in['b_qkv'], 'L0_attn_w_proj': _L0_attn_in['w_proj'], 'L0_attn_b_proj': _L0_attn_in['b_proj'], 'L0_ffn_router_w': _L0_ffn_in['router_w'], 'L0_ffn_router_bias': _L0_ffn_in['router_bias'], 'L0_ffn_wg': _L0_ffn_in['wg'], 'L0_ffn_wu': _L0_ffn_in['wu'], 'L0_ffn_wd': _L0_ffn_in['wd'], 'L0_ffn_swg': _L0_ffn_in['swg'], 'L0_ffn_swu': _L0_ffn_in['swu'], 'L0_ffn_swd': _L0_ffn_in['swd'], 'L1_attn_W_in': _L1_attn_in['W_in'], 'L1_attn_conv_w': _L1_attn_in['conv_w'], 'L1_attn_conv_b': _L1_attn_in['conv_b'], 'L1_attn_A_log': _L1_attn_in['A_log'], 'L1_attn_D_param': _L1_attn_in['D_param'], 'L1_attn_dt_bias': _L1_attn_in['dt_bias'], 'L1_attn_W_out': _L1_attn_in['W_out'], 'L1_ffn_W0': _L1_ffn_in['W0'], 'L1_ffn_bias0': _L1_ffn_in['bias0'], 'L1_ffn_W1': _L1_ffn_in['W1'], 'L1_ffn_bias1': _L1_ffn_in['bias1']}
    _x0 = _d['L0_attn_hidden_states']
    _d['L0_attn_hidden_states'] = jax.random.normal(jax.random.fold_in(jax.random.key(seed), 1), (8, 256, 256), dtype=_x0.dtype)
    del _x0
    return _d

def reference(L0_attn_hidden_states, L0_attn_w_qkv, L0_attn_b_qkv, L0_attn_w_proj, L0_attn_b_proj, L0_ffn_router_w, L0_ffn_router_bias, L0_ffn_wg, L0_ffn_wu, L0_ffn_wd, L0_ffn_swg, L0_ffn_swu, L0_ffn_swd, L1_attn_W_in, L1_attn_conv_w, L1_attn_conv_b, L1_attn_A_log, L1_attn_D_param, L1_attn_dt_bias, L1_attn_W_out, L1_ffn_W0, L1_ffn_bias0, L1_ffn_W1, L1_ffn_bias1):

    def _L0_attn_ref(hidden_states, w_qkv, b_qkv, w_proj, b_proj):
        import math
        import jax, jax.numpy as jnp
        import numpy as np

        def _alibi_slopes(n):

            def pow2_slopes(n):
                start = 2.0 ** (-2.0 ** (-(math.log2(n) - 3)))
                return [start * start ** i for i in range(n)]
            if math.log2(n).is_integer():
                return pow2_slopes(n)
            cp2 = 2 ** math.floor(math.log2(n))
            return pow2_slopes(cp2) + _alibi_slopes(2 * cp2)[0::2][:n - cp2]
        NUM_HEADS = 16
        B, S, H = hidden_states.shape
        nh = NUM_HEADS
        hd = H // nh
        scale = 1.0 / hd
        qkv = hidden_states @ w_qkv + b_qkv
        q, k, v = jnp.split(qkv, 3, axis=-1)
        q = q.reshape(B, S, nh, hd)
        k = k.reshape(B, S, nh, hd)
        v = v.reshape(B, S, nh, hd)
        scores = jnp.einsum('bqhd,bkhd->bhqk', q, k) * scale
        slopes = jnp.asarray(_alibi_slopes(nh), dtype=scores.dtype)
        pos = jnp.arange(S)
        rel = (pos[None, :] - pos[:, None]).astype(scores.dtype)
        bias = slopes[:, None, None] * rel[None, :, :]
        causal = pos[None, :] <= pos[:, None]
        scores = jnp.where(causal[None, None], scores + bias[None], jnp.finfo(scores.dtype).min)
        attn = jax.nn.softmax(scores, axis=-1)
        out = jnp.einsum('bhqk,bkhd->bqhd', attn, v).reshape(B, S, H)
        return out @ w_proj + b_proj

    def _L0_ffn_ref(x, router_w, router_bias, wg, wu, wd, swg, swu, swd):
        import jax, jax.numpy as jnp
        import numpy as np
        B, T, D = (2, 128, 256)
        E, F, K = (64, 64, 4)
        S, HS = (2, 64 * 4)
        b, t, d = x.shape
        flat = x.reshape(b * t, d)
        n = flat.shape[0]
        logits = flat @ router_w
        scores = jax.nn.softmax(logits, axis=-1)
        _, topk_idx = jax.lax.top_k(logits + router_bias, K)
        topk_scores = jnp.take_along_axis(scores, topk_idx, axis=-1)
        topk_scores = topk_scores / topk_scores.sum(axis=-1, keepdims=True)
        comb = jnp.zeros((n, E), dtype=flat.dtype).at[jnp.arange(n)[:, None], topk_idx].set(topk_scores)
        g = jax.nn.silu(jnp.einsum('nd,edf->nef', flat, wg))
        u = jnp.einsum('nd,edf->nef', flat, wu)
        routed = jnp.einsum('ne,nef,efd->nd', comb, g * u, wd)
        sg = jax.nn.silu(jnp.einsum('nd,sdh->nsh', flat, swg))
        su = jnp.einsum('nd,sdh->nsh', flat, swu)
        shared = jnp.einsum('nsh,shd->nd', sg * su, swd)
        return (routed + shared).reshape(b, t, d)

    def _L1_attn_ref(x, W_in, conv_w, conv_b, A_log, D_param, dt_bias, W_out):
        import jax, jax.numpy as jnp
        import numpy as np
        B, L, DM = (2, 256, 256)
        EXPAND, D_STATE, D_CONV, H, CS = (2, 128, 4, 32, 32)
        D_INNER = EXPAND * DM
        HD = D_INNER // H
        N = D_STATE
        PROJ = 2 * D_INNER + 2 * H * N + H
        b, l, _ = x.shape
        proj = x @ W_in.T
        val, gate, Bp, Cp, dt = jnp.split(proj, [D_INNER, 2 * D_INNER, 2 * D_INNER + H * N, 2 * D_INNER + 2 * H * N], axis=-1)
        vc = jax.lax.conv_general_dilated(val.transpose(0, 2, 1), conv_w, (1,), [(D_CONV - 1, 0)], dimension_numbers=('NCH', 'OIH', 'NCH'), feature_group_count=D_INNER)
        val = jax.nn.silu(vc.transpose(0, 2, 1) + conv_b)
        val = val.reshape(b, l, H, HD)
        Bp = Bp.reshape(b, l, H, N)
        Cp = Cp.reshape(b, l, H, N)
        dt = jax.nn.softplus(dt + dt_bias)
        ld = dt * -jnp.exp(A_log)
        nC = l // CS
        mask = jnp.tril(jnp.ones((CS, CS), bool))
        Dh = D_param.reshape(1, H, 1, HD)

        def chunk(h, inp):
            val_c, B_c, C_c, ld_c = inp
            cum = jnp.cumsum(ld_c, axis=1)
            cumh = cum.transpose(0, 2, 1)
            diff = jnp.where(mask, cumh[:, :, :, None] - cumh[:, :, None, :], -jnp.inf)
            CB = jnp.einsum('blhn,bmhn->bhlm', C_c, B_c)
            M = CB * jnp.exp(diff)
            val_ch = val_c.transpose(0, 2, 1, 3)
            Y = M @ val_ch + jnp.einsum('blhn,bhdn,blh->bhld', C_c, h, jnp.exp(cum)) + Dh * val_ch
            last = cum[:, -1, :]
            h_new = jnp.exp(last)[:, :, None, None] * h + jnp.einsum('blhd,blhn,blh->bhdn', val_c, B_c, jnp.exp(last[:, None, :] - cum))
            return (h_new, Y)
        inps = tuple((jnp.moveaxis(a.reshape(b, nC, CS, *a.shape[2:]), 1, 0) for a in (val, Bp, Cp, ld)))
        h0 = jnp.zeros((b, H, HD, N), jnp.float32)
        _, Ys = jax.lax.scan(chunk, h0, inps)
        Y = Ys.transpose(1, 0, 3, 2, 4).reshape(b, l, D_INNER)
        Y = Y * jax.nn.silu(gate)
        return Y @ W_out.T

    def _L1_ffn_ref(x, W0, bias0, W1, bias1):
        import jax, jax.numpy as jnp
        import numpy as np
        B, L, H = x.shape
        X = x.reshape(-1, H).astype(jnp.float16)
        D = jnp.dot(X.astype(jnp.float32), W0.T) + bias0
        D = jax.nn.gelu(D, approximate=False).astype(jnp.float16)
        E = jnp.dot(D.astype(jnp.float32), W1.T) + bias1
        return E.astype(jnp.float16).reshape(B, L, H)
    x = L0_attn_hidden_states
    x = x + _layernorm(_L0_attn_ref(_layernorm(x, axis=-1), L0_attn_w_qkv, L0_attn_b_qkv, L0_attn_w_proj, L0_attn_b_proj), axis=-1)
    x = x + _layernorm(_L0_ffn_ref(_layernorm(x, axis=-1), L0_ffn_router_w, L0_ffn_router_bias, L0_ffn_wg, L0_ffn_wu, L0_ffn_wd, L0_ffn_swg, L0_ffn_swu, L0_ffn_swd), axis=-1)
    x = x + _layernorm(_L1_attn_ref(_layernorm(x, axis=-1), L1_attn_W_in, L1_attn_conv_w, L1_attn_conv_b, L1_attn_A_log, L1_attn_D_param, L1_attn_dt_bias, L1_attn_W_out), axis=-1)
    x = x + _layernorm(_L1_ffn_ref(_layernorm(x, axis=-1), L1_ffn_W0, L1_ffn_bias0, L1_ffn_W1, L1_ffn_bias1), axis=-1)
    return x

_drawn_inputs = setup_inputs


def setup_inputs(seed=0):
    import zlib

    import numpy as np

    out = dict(_drawn_inputs(seed))
    spreads = {'L0_ffn_router_bias': (0.0, 0.1),
     'L1_attn_conv_b': (0.0, 0.1),
     'L1_attn_A_log': (0.6931471824645996, 0.59),
     'L1_attn_D_param': (1.0, 0.2),
     'L1_attn_dt_bias': (0.0, 0.753)}
    factors = {'L1_ffn_bias0': 6.191, 'L1_ffn_bias1': 4.331}
    for name, (base, spread) in spreads.items():
        noise = np.random.default_rng([zlib.crc32(name.encode()), seed]).standard_normal(out[name].shape)
        drawn = base * np.exp(spread * noise) if base else spread * noise
        out[name] = jnp.asarray(drawn.astype(out[name].dtype))
    for name, factor in factors.items():
        out[name] = (out[name] * factor).astype(out[name].dtype)
    return out
```

```python
from contextlib import ExitStack

import concourse.bass as bass
from concourse import mybir

F32 = mybir.dt.float32
F32R = mybir.dt.float32r
BF16 = mybir.dt.bfloat16
F16 = mybir.dt.float16
ALU = mybir.AluOpType
ACT = mybir.ActivationFunctionType
AX = mybir.AxisListType

P = 128
D = 256
KD = D // P
B, S = 8, 256
NT = B * S // P
TOK = B * S
EPS = 1e-5

NH, HD = 16, 16
HPG = 4
NG = NH // HPG
HROW = 32
KROW = HD + 1

NE, FE, TOPK = 64, 64, 4
ROUTED = NE * FE // P
SHARED = 4
WBLK = 3 * D
BIG = 3.0e38

SH, SHD, SN = 32, 16, 128
DI = SH * SHD
NC = DI // P
CHUNK = 512
NCH = TOK // CHUNK
TPC = CHUNK // P

FH = 1024
NFH = FH // P


class Chip:

    def __init__(self, nc, sems):
        self.nc, self.sems, self.count = nc, sems, 0

    def sem(self, name):
        self.count += 1
        return self.sems.enter_context(self.nc.semaphore(f"{name}_{self.count}"))

    def memory(self, ctx):
        def sb(name, shape, dt=F32):
            self.count += 1
            return ctx.enter_context(self.nc.sbuf_tensor(f"{name}_{self.count}", shape, dt))

        def pb(name, shape):
            self.count += 1
            return ctx.enter_context(self.nc.psum_tensor(f"{name}_{self.count}", shape, F32))

        return sb, pb


def linker(eng, sem):
    n = [0]

    def link(ins):
        n[0] += 1
        ins.then_inc(sem, 1)
        eng.wait_ge(sem, n[0])

    return link


def repeat(eng, times, body):
    body(0)
    with eng.Fori(1, times) as i:
        body(i)


def after(eng, sem, value):
    if not isinstance(value, int) or value > 0:
        eng.wait_ge(sem, value)


def flat(ap):
    return ap.rearrange("p a b -> p (a b)")



def stage_norm(chip, x, y, xh, xl, ident, add_y, make_norm, half=False, x_loaded=None, out=None):
    nc = chip.nc
    with ExitStack() as ctx:
        sb, pb = chip.memory(ctx)

        stats = sb("stats", [P, NT, 6])
        small = sb("small", [P, 6, NT])
        power = sb("power", [P, NT])
        mean = [sb(f"mean{n}", [P, NT]) for n in range(2)]
        var = [sb(f"var{n}", [P, NT]) for n in range(2)]
        rstd = [sb(f"rstd{n}", [P, NT]) for n in range(2)]
        xn = sb("xn", [P, 2, 2, D])
        xn16 = sb("xn16", [P, 2, 2, D], F16)
        turned = [pb(f"turned{n}", [P, KD, S]) for n in range(2)]
        chain = chip.sem("norm_chain")
        power_set = chip.sem("power_set")
        var_ready = chip.sem("var_ready")
        rstd_ready = chip.sem("rstd_ready")
        xn_ready = chip.sem("xn_ready")
        xn_turned = chip.sem("xn_turned")
        hi_ready = chip.sem("hi_ready")
        lo_ready = chip.sem("lo_ready")
        x_final = chip.sem("x_final")
        stored = chip.sem("stored")
        norms = [n for n in range(2) if (add_y, make_norm)[n]]
        with nc.Block() as block:
            @block.gpsimd
            def _(pool):
                nc.gpsimd.memset(power[:], -0.5).then_inc(power_set, 1)
                pool.wait_ge(power_set, 1)
                for n, norm in enumerate(norms):
                    pool.wait_ge(var_ready, n + 1)
                    nc.gpsimd.tensor_tensor(rstd[norm][:], var[norm][:], power[:], ALU.pow).then_inc(rstd_ready, 1)

            @block.vector
            def _(dve):
                link = linker(dve, chain)
                if x_loaded is not None:
                    dve.wait_ge(*x_loaded)

                def statistics(src, norm):
                    for t in range(NT):
                        last = nc.vector.bn_stats(stats[:, t, :], src[:, t, :])
                    link(last)
                    even_mean, even_m2 = stats[:, :, 1], stats[:, :, 2]
                    odd_mean, odd_m2 = stats[:, :, 4], stats[:, :, 5]
                    nc.vector.tensor_tensor(small[:, 0, :], even_mean, odd_mean, ALU.add)
                    nc.vector.tensor_tensor(small[:, 2, :], even_m2, odd_m2, ALU.add)
                    link(nc.vector.tensor_tensor(small[:, 1, :], even_mean, odd_mean, ALU.subtract))
                    nc.vector.tensor_scalar(mean[norm][:], small[:, 0, :], 0.5, None, ALU.mult)
                    link(nc.vector.tensor_tensor(small[:, 3, :], small[:, 1, :], small[:, 1, :], ALU.mult))
                    link(nc.vector.scalar_tensor_tensor(small[:, 4, :], small[:, 3, :], D / 4.0, small[:, 2, :],
                                                        ALU.mult, ALU.add))
                    nc.vector.tensor_scalar(var[norm][:], small[:, 4, :], 1.0 / D, EPS, ALU.mult,
                                            ALU.add).then_inc(var_ready, 1)

                def scaled(dst, src, norm, t):
                    return nc.vector.tensor_scalar(dst, src, mean[norm][:, t:t + 1], rstd[norm][:, t:t + 1],
                                                   ALU.subtract, ALU.mult)

                if add_y:
                    statistics(y, 0)
                    dve.wait_ge(rstd_ready, 1)
                    for t in range(NT):
                        last = scaled(y[:, t, :], y[:, t, :], 0, t)
                    link(last)
                    ins = nc.vector.tensor_tensor(flat(x[:]), flat(x[:]), flat(y[:]), ALU.add)
                    if make_norm:
                        link(ins)
                    else:
                        ins.then_inc(x_final, 1)
                if make_norm:
                    statistics(x, 1)
                    dve.wait_ge(rstd_ready, len(norms))
                    for b in range(B + 1):
                        if b < B:
                            dst = xn16 if half else xn
                            scaled(dst[:, b % 2, 0, :], x[:, 2 * b, :], 1, 2 * b)
                            last = scaled(dst[:, b % 2, 1, :], x[:, 2 * b + 1, :], 1, 2 * b + 1)
                            if half:
                                link(last)
                                last = nc.vector.tensor_copy(xn[:, b % 2, :, :], xn16[:, b % 2, :, :])
                            last.then_inc(xn_ready, 1)
                        if b >= 1 and half:
                            dve.wait_ge(xn_turned, b)
                        if b >= 1 and not half:
                            dve.wait_ge(hi_ready, b)
                            nc.vector.tensor_tensor(xl[:, :, (b - 1) * S:b * S], turned[(b - 1) % 2][:],
                                                    xh[:, :, (b - 1) * S:b * S].bitcast(F32),
                                                    ALU.subtract).then_inc(lo_ready, 1)

            if make_norm:
                @block.tensor
                def _(pe):
                    for b in range(B):
                        pe.wait_ge(xn_ready, b + 1)
                        if b >= 2:
                            pe.wait_ge(hi_ready if half else lo_ready, b - 1)
                        for t in range(2):
                            for k in range(KD):
                                last = nc.tensor.transpose(turned[b % 2][:, k, t * P:(t + 1) * P],
                                                           xn[:, b % 2, t, k * P:(k + 1) * P], ident[:])
                        last.then_inc(xn_turned, 1)

                @block.scalar
                def _(act):
                    for b in range(B):
                        act.wait_ge(xn_turned, b + 1)
                        nc.scalar.activation(xh[:, :, b * S:(b + 1) * S], turned[b % 2][:],
                                             ACT.Copy).then_inc(hi_ready, 1)

            if out is not None:
                @block.sync
                def _(sp):
                    sp.wait_ge(x_final, 1)
                    sp.dma_start(out, x[:]).then_inc(stored, 16)
                    sp.wait_ge(stored, 16)



QK_BANKS = 4
RING = 3
USES = 24
U_V, U_HEAD, U_TURN, U_PROJ = QK_BANKS, QK_BANKS + 1, QK_BANKS + 1 + NH, QK_BANKS + 2 + NH


def stage_attention(chip, xh, xl, y, ident, ins):
    nc = chip.nc
    with ExitStack() as ctx:
        sb, pb = chip.memory(ctx)

        wraw = sb("wraw", [P, KD, 2 * NG * P + D])
        wh = sb("wh", [P, KD, 2 * NG * P + D], F32R)
        wl = sb("wl", [P, KD, 2 * NG * P + D], F32R)
        wproj = sb("wproj", [P, KD, D])
        bqk = sb("bqk", [P, 2 * NG])
        bv = sb("bv", [P, D])
        bproj = sb("bproj", [P, D])
        ramp = sb("ramp", [P, S])
        identb = sb("identb", [P, P], BF16)
        mask = sb("mask", [P, P], BF16)
        xs = sb("xs", [P, 2, KD, S], F32R)
        qT = sb("qT", [P, NG, S])
        kT = sb("kT", [P, NG, S])
        v1 = sb("v1", [P, 2, NH, KROW])
        negmax = sb("negmax", [P, RING, 2])
        prob = sb("prob", [P, RING, 3 * P])
        probT = sb("probT", [P, RING, 3 * P])
        rsum = sb("rsum", [P, 2, NH])
        on = sb("on", [P, 2, D])
        oT = sb("oT", [P, KD, S])
        work = [pb(f"work{n}", [P, 512]) for n in range(RING)]
        pturn = [pb(f"pturn{n}", [P, 512]) for n in range(2)]
        acc = [pb(f"acc{n}", [P, 512]) for n in range(2)]
        acc_h = [a[:, 0:NH * KROW].rearrange("p (h c) -> p h c", c=KROW) for a in acc]

        loaded, raw_loaded = chip.sem("loaded"), chip.sem("raw_loaded")
        split_done, ones_set = chip.sem("split_done"), chip.sem("ones_set")
        x_staged = chip.sem("x_staged")
        filled = chip.sem("filled")
        emptied = chip.sem("emptied")
        scored = chip.sem("scored")
        maxed = chip.sem("maxed")
        exped = chip.sem("exped")
        p_turned = chip.sem("p_turned")
        p_copied = chip.sem("p_copied")
        pv_done = chip.sem("pv_done")
        inverted = chip.sem("inverted")
        normed = chip.sem("normed")
        o_turned = chip.sem("o_turned")
        o_copied = chip.sem("o_copied")
        projected = chip.sem("projected")
        y_ready = chip.sem("y_ready")
        NQ = 2 * NG * P

        with nc.Block() as block:
            @block.sync
            def _(sp):
                sp.dma_start(wraw[:], ins["wqkv"]).then_inc(raw_loaded, 16)
                for dst, src in ((bqk, "bqk"), (bv, "bv"), (bproj, "bproj"), (ramp, "ramp"),
                                 (identb, "identb"), (mask, "causal_add"), (wproj, "wproj")):
                    sp.dma_start(dst[:], ins[src]).then_inc(loaded, 16)

            @block.gpsimd
            def _(pool):
                nc.gpsimd.memset(v1[:], 1.0).then_inc(ones_set, 1)
                def body(b):
                    after(pool, filled, b * 5)
                    nc.gpsimd.tensor_copy(xs[:, 0, :, :], xh[:, :, bass.ts(b, S)].bitcast(F32))
                    nc.gpsimd.tensor_copy(xs[:, 1, :, :], xl[:, :, bass.ts(b, S)].bitcast(F32)).then_inc(x_staged, 1)

                repeat(pool, B, body)

            @block.tensor
            def _(pe):
                pe.wait_ge(split_done, 2)
                pe.wait_ge(loaded, 7 * 16)
                def body(b):
                    pe.wait_ge(x_staged, b + 1)
                    for u in range(QK_BANKS):
                        if u == 1:
                            after(pe, y_ready, b)
                        if u == 3:
                            pe.wait_ge(emptied, b * 5 + 1)
                        for n in range(2):
                            cols = slice((2 * u + n) * P, (2 * u + n + 1) * P)
                            parts = [(w, a, k) for k in range(KD) for w, a in ((wh, 0), (wh, 1), (wl, 0))]
                            for m, (w, a, k) in enumerate(parts):
                                last = nc.tensor.matmul(work[u % RING][:, n * S:(n + 1) * S], w[:, k, cols],
                                                        xs[:, a, k, :], start=(m == 0), stop=(m == len(parts) - 1))
                        last.then_inc(filled, 1)
                    pe.wait_ge(emptied, b * 5 + 2)
                    for t in range(2):
                        parts = [(w, a, k) for k in range(KD) for a, w in ((0, wh), (0, wl), (1, wh))]
                        for m, (w, a, k) in enumerate(parts):
                            last = nc.tensor.matmul(work[U_V % RING][:, t * D:(t + 1) * D],
                                                    xs[:, a, k, t * P:(t + 1) * P], w[:, k, NQ:],
                                                    start=(m == 0), stop=(m == len(parts) - 1))
                    last.then_inc(filled, 1)
                    for s in range(NH + 3):
                        if s < NH:
                            h, bank = s, work[(U_HEAD + s) % RING]
                            if s == 0:
                                pe.wait_ge(emptied, b * 5 + 4)
                            if s == 2:
                                pe.wait_ge(emptied, b * 5 + 5)
                            if s >= 3:
                                pe.wait_ge(exped, b * NH + s - 2)
                            r0, g = (h % HPG) * HROW, h // HPG
                            rows = slice(r0, r0 + KROW)
                            nc.tensor.matmul(bank[:, 0:P], qT[rows, g, 0:P], kT[rows, g, 0:P], start=True, stop=False)
                            nc.tensor.matmul(bank[:, 0:P], identb[:], mask[:], start=False, stop=True)
                            nc.tensor.matmul(bank[:, P:3 * P], qT[rows, g, P:S], kT[rows, g, :],
                                             start=True, stop=False)
                            nc.tensor.matmul(bank[:, 2 * P:3 * P], identb[:], mask[:], start=False,
                                             stop=True).then_inc(scored, 1)
                        if 2 <= s < NH + 2:
                            h = s - 2
                            pe.wait_ge(exped, b * NH + h + 1)
                            if h >= 2:
                                pe.wait_ge(p_copied, b * NH + h - 1)
                            for n in range(3):
                                last = nc.tensor.transpose(pturn[h % 2][:, n * P:(n + 1) * P],
                                                           prob[:, h % RING, n * P:(n + 1) * P], ident[:])
                            last.then_inc(p_turned, 1)
                        if s >= 3:
                            h = s - 3
                            pe.wait_ge(p_copied, b * NH + h + 1)
                            if h == 0:
                                pe.wait_ge(emptied, b * 5 + 5)
                            nc.tensor.matmul(acc_h[0][:, h, :], probT[:, h % RING, 0:P], v1[:, 0, h, :],
                                             start=True, stop=True)
                            nc.tensor.matmul(acc_h[1][:, h, :], probT[:, h % RING, P:2 * P], v1[:, 0, h, :],
                                             start=True, stop=False)
                            nc.tensor.matmul(acc_h[1][:, h, :], probT[:, h % RING, 2 * P:3 * P], v1[:, 1, h, :],
                                             start=False, stop=True).then_inc(pv_done, 1)
                    pe.wait_ge(normed, b + 1)
                    for t in range(2):
                        for k in range(KD):
                            last = nc.tensor.transpose(work[U_TURN % RING][:, k * S + t * P:k * S + (t + 1) * P],
                                                       on[:, t, k * P:(k + 1) * P], ident[:])
                    last.then_inc(o_turned, 1)
                    pe.wait_ge(o_copied, b + 1)
                    for t in range(2):
                        for k in range(KD):
                            last = nc.tensor.matmul(work[U_PROJ % RING][:, t * D:(t + 1) * D],
                                                    oT[:, k, t * P:(t + 1) * P], wproj[:, k, :],
                                                    start=(k == 0), stop=(k == KD - 1))
                    last.then_inc(projected, 1)

                repeat(pe, B, body)

            @block.scalar
            def _(act):
                def body(b):
                    for h in range(NH):
                        act.wait_ge(maxed, b * NH + h + 1)
                        if h >= RING:
                            act.wait_ge(p_turned, b * NH + h - RING + 1)
                        bank = work[(U_HEAD + h) % RING]
                        nc.scalar.activation(prob[:, h % RING, 0:P], bank[:, 0:P], ACT.Exp,
                                             bias=negmax[:, h % RING, 0:1])
                        nc.scalar.activation(prob[:, h % RING, P:3 * P], bank[:, P:3 * P], ACT.Exp,
                                             bias=negmax[:, h % RING, 1:2]).then_inc(exped, 1)
                    act.wait_ge(o_turned, b + 1)
                    nc.scalar.activation(flat(oT[:]), work[U_TURN % RING][:], ACT.Copy).then_inc(o_copied, 1)

                repeat(act, B, body)

            @block.vector
            def _(dve):
                dve.wait_ge(raw_loaded, 16)
                nc.vector.tensor_copy(flat(wh[:]), flat(wraw[:])).then_inc(split_done, 1)
                dve.wait_ge(split_done, 1)
                nc.vector.tensor_tensor(flat(wl[:]), flat(wraw[:]), flat(wh[:]).bitcast(F32),
                                        ALU.subtract).then_inc(split_done, 1)
                dve.wait_ge(loaded, 7 * 16)
                dve.wait_ge(ones_set, 1)
                def body(b):
                    for u in range(QK_BANKS):
                        dve.wait_ge(filled, b * 5 + u + 1)
                        for n in range(2):
                            g = (2 * u + n) % NG
                            src = work[u % RING][:, n * S:(n + 1) * S]
                            bias = bqk[:, 2 * u + n:2 * u + n + 1]
                            if u < QK_BANKS // 2:
                                last = nc.vector.tensor_scalar(qT[:, g, :], src, bias, 1.0 / HD, ALU.add, ALU.mult)
                            else:
                                last = nc.vector.scalar_tensor_tensor(kT[:, g, :], src, bias, ramp[:],
                                                                      ALU.add, ALU.add)
                        last.then_inc(emptied, 1)
                    dve.wait_ge(filled, b * 5 + 5)
                    for t in range(2):
                        last = nc.vector.tensor_tensor(
                            v1[:, t, :, 0:HD],
                            work[U_V % RING][:, t * D:(t + 1) * D].rearrange("p (h c) -> p h c", c=HD),
                            bv[:].rearrange("p (h c) -> p h c", c=HD), ALU.add)
                    last.then_inc(emptied, 1)
                    for s in range(NH + 2):
                        if s < NH:
                            bank = work[(U_HEAD + s) % RING]
                            dve.wait_ge(scored, b * NH + s + 1)
                            nc.vector.tensor_reduce(negmax[:, s % RING, 0:1], bank[:, 0:P], AX.X, ALU.max,
                                                    negate=True)
                            nc.vector.tensor_reduce(negmax[:, s % RING, 1:2], bank[:, P:3 * P], AX.X, ALU.max,
                                                    negate=True).then_inc(maxed, 1)
                        if s >= 2:
                            h = s - 2
                            dve.wait_ge(p_turned, b * NH + h + 1)
                            if h >= RING:
                                dve.wait_ge(pv_done, b * NH + h - RING + 1)
                            nc.vector.tensor_copy(probT[:, h % RING, :],
                                                  pturn[h % 2][:, 0:3 * P]).then_inc(p_copied, 1)
                    dve.wait_ge(pv_done, b * NH + NH)
                    for t in range(2):
                        nc.vector.reciprocal(rsum[:, t, :], acc_h[t][:, :, HD]).then_inc(inverted, 1)
                    dve.wait_ge(inverted, b * 2 + 2)
                    for t in range(2):
                        last = nc.vector.tensor_tensor(
                            on[:, t, :].rearrange("p (h c) -> p h c", c=HD), acc_h[t][:, :, 0:HD],
                            rsum[:, t, :].unsqueeze(2).broadcast_to([P, NH, HD]), ALU.mult)
                    last.then_inc(normed, 1)
                    dve.wait_ge(projected, b + 1)
                    bank = work[U_PROJ % RING]
                    ydst = y[:, bass.ts(b, 2), :]
                    nc.vector.tensor_tensor(ydst, bank[:, :].rearrange("p (t n) -> p t n", n=D),
                                            bproj[:].unsqueeze(1).broadcast_to([P, 2, D]),
                                            ALU.add).then_inc(y_ready, 1)

                repeat(dve, B, body)



GROUPS = 2
GCH = NCH // GROUPS
GT = NT // GROUPS


def stage_moe(chip, xh, xl, y, ident, ins):
    nc = chip.nc
    with ExitStack() as outer:
        sb, _ = chip.memory(outer)
        combT = sb("combT", [P, TOK], F32R)
        stage_router(chip, xh, xl, combT, ident, ins)
        stage_experts(chip, xh, xl, combT, y, ins)


def stage_router(chip, xh, xl, combT, ident, ins):
    nc = chip.nc
    TB = 8
    with ExitStack() as ctx:
        sb, pb = chip.memory(ctx)
        wraw = sb("wraw", [P, KD, NE])
        wh = sb("wh", [P, KD, NE], F32R)
        wl = sb("wl", [P, KD, NE], F32R)
        bias = sb("bias", [P, NE])
        logit = sb("logit", [P, NT, NE])
        ranked = sb("ranked", [P, NT, NE + TOPK])
        best = sb("best", [P, NT, 8])
        left = sb("left", [P, NT, NE + TOPK])
        chosen = sb("chosen", [P, NT, NE])
        expd = sb("expd", [P, NT, NE])
        top = sb("top", [P, NT])
        total = sb("total", [P, NT])
        inv = sb("inv", [P, NT])
        ps = [pb(f"logits{n}", [P, TB, NE]) for n in range(2)]
        pt = [pb(f"combined{n}", [P, CHUNK]) for n in range(2)]
        loaded, chain = chip.sem("loaded"), chip.sem("router_chain")
        split_done, logits_done = chip.sem("split_done"), chip.sem("logits_done")
        shifted, exp_done = chip.sem("shifted"), chip.sem("exp_done")
        comb_done, turned = chip.sem("comb_done"), chip.sem("turned")
        hi_done, lo_done = chip.sem("hi_done"), chip.sem("lo_done")
        with nc.Block() as block:
            @block.sync
            def _(sp):
                sp.dma_start(wraw[:], ins["router_w"]).then_inc(loaded, 16)
                sp.dma_start(bias[:], ins["router_b"]).then_inc(loaded, 16)

            @block.tensor
            def _(pe):
                pe.wait_ge(split_done, 2)
                parts = [(a, w, k) for k in range(KD) for a, w in ((xh, wh), (xh, wl), (xl, wh))]
                for t in range(NT):
                    for m, (a, w, k) in enumerate(parts):
                        last = nc.tensor.matmul(ps[t // TB][:, t % TB, :], a[:, k, t * P:(t + 1) * P], w[:, k, :],
                                                start=(m == 0), stop=(m == len(parts) - 1))
                    if t % TB == TB - 1:
                        last.then_inc(logits_done, 1)
                pe.wait_ge(comb_done, 1)
                for c in range(NCH):
                    if c >= 2:
                        pe.wait_ge(lo_done, c - 1)
                    for n in range(TPC):
                        last = nc.tensor.transpose(pt[c % 2][0:NE, n * P:(n + 1) * P], expd[:, c * TPC + n, :],
                                                   ident[:])
                    last.then_inc(turned, 1)

            @block.scalar
            def _(act):
                act.wait_ge(shifted, 1)
                nc.scalar.activation(flat(expd[:]), flat(logit[:]), ACT.Exp).then_inc(exp_done, 1)

            @block.vector
            def _(dve):
                link = linker(dve, chain)
                dve.wait_ge(loaded, 32)
                nc.vector.tensor_copy(flat(wh[:]), flat(wraw[:])).then_inc(split_done, 1)
                dve.wait_ge(split_done, 1)
                nc.vector.tensor_tensor(flat(wl[:]), flat(wraw[:]), flat(wh[:]).bitcast(F32),
                                        ALU.subtract).then_inc(split_done, 1)
                nc.vector.memset(ranked[:, :, NE:], BIG)
                for n in range(NT // TB):
                    tiles = slice(n * TB, (n + 1) * TB)
                    dve.wait_ge(logits_done, n + 1)
                    nc.vector.tensor_copy(logit[:, tiles, :], ps[n][:])
                    link(nc.vector.tensor_tensor(ranked[:, tiles, 0:NE], ps[n][:],
                                                 bias[:].unsqueeze(1).broadcast_to([P, TB, NE]), ALU.add))
                link(nc.vector.tensor_reduce(top[:], logit[:], AX.X, ALU.max))
                link(nc.vector.tensor_tensor(logit[:], logit[:], top[:].unsqueeze(2).broadcast_to([P, NT, NE]),
                                             ALU.subtract))
                nc.vector.sem_inc(shifted, 1)
                for t in range(NT):
                    last = nc.vector.max(best[:, t, :], ranked[:, t, :])
                link(last)
                for t in range(NT):
                    last = nc.vector.match_replace(left[:, t, :], best[:, t, :], ranked[:, t, :], -BIG)
                link(last)
                link(nc.vector.tensor_tensor(chosen[:], ranked[:, :, 0:NE], left[:, :, 0:NE], ALU.not_equal))
                dve.wait_ge(exp_done, 1)
                link(nc.vector.tensor_tensor(flat(expd[:]), flat(expd[:]), flat(chosen[:]), ALU.mult))
                link(nc.vector.tensor_reduce(total[:], expd[:], AX.X, ALU.add))
                link(nc.vector.reciprocal(inv[:], total[:]))
                nc.vector.tensor_tensor(expd[:], expd[:], inv[:].unsqueeze(2).broadcast_to([P, NT, NE]),
                                        ALU.mult).then_inc(comb_done, 1)
                for c in range(NCH):
                    cols = slice(c * CHUNK, (c + 1) * CHUNK)
                    dve.wait_ge(turned, c + 1)
                    nc.vector.tensor_copy(combT[0:NE, cols], pt[c % 2][0:NE, :]).then_inc(hi_done, 1)
                    dve.wait_ge(hi_done, c + 1)
                    nc.vector.tensor_tensor(combT[NE:2 * NE, cols], pt[c % 2][0:NE, :],
                                            combT[0:NE, cols].bitcast(F32), ALU.subtract).then_inc(lo_done, 1)


def stage_experts(chip, xh, xl, combT, y, ins):
    nc = chip.nc
    WCOL = WBLK + P
    TURNS_R, TURNS_S = ROUTED // 2, SHARED // 2
    TURNS = TURNS_R + TURNS_S
    STEPS = 2 * GCH
    with ExitStack() as ctx:
        sb, pb = chip.memory(ctx)
        wraw = sb("wraw", [P, 2, WCOL])
        wh = sb("wh", [P, 2, WCOL], F32R)
        wl = sb("wl", [P, 2, WBLK], F32R)
        gate = sb("gate", [P, 2, CHUNK])
        prod = sb("prod", [P, 2, CHUNK])
        hid = sb("hid", [P, 2, CHUNK])
        hh = sb("hh", [P, 2, CHUNK], F32R)
        hl = sb("hl", [P, 2, CHUNK], F32R)
        zeros = sb("zeros", [P, CHUNK], BF16)
        none = sb("none", [P, 1])
        pg, pu, pc = pb("pg", [P, CHUNK]), pb("pu", [P, CHUNK]), pb("pc", [P, CHUNK])
        acc = [pb(f"acc{n}", [P, 2, D]) for n in range(GT // 2)]
        zeroed, none_set = chip.sem("zeroed"), chip.sem("none_set")
        w_loaded = [chip.sem("w_loaded") for _ in range(2)]
        w_half, w_split = chip.sem("w_half"), chip.sem("w_split")
        gate_done, up_done, comb_done = chip.sem("gate_done"), chip.sem("up_done"), chip.sem("comb_done")
        silu_done, prod_done, hid_done = chip.sem("silu_done"), chip.sem("prod_done"), chip.sem("hid_done")
        hi_done, lo_done = chip.sem("hi_done"), chip.sem("lo_done")
        down_done, y_out = chip.sem("down_done"), chip.sem("y_out")

        def turns(eng, body):
            for g in range(GROUPS):
                body(g * TURNS, g, True, True)
                with eng.Fori(g * TURNS + 1, g * TURNS + TURNS_R) as i:
                    body(i, g, True, False)
                with eng.Fori(g * TURNS + TURNS_R, (g + 1) * TURNS) as i:
                    body(i, g, False, False)
                yield g

        with nc.Block() as block:
            @block.sync
            def _(sp):
                def load(i, g):
                    for s in range(2):
                        if g or not isinstance(i, int):
                            sp.wait_ge(w_split, (i + g * TURNS) * 2 + (s - 1))
                        sp.dma_start(wraw[:, s, :], ins["experts"][bass.ds(i * 2 + s, 1), :, :]
                                     .rearrange("a p n -> p (a n)")).then_inc(w_loaded[s], 16)

                for g in range(GROUPS):
                    load(0, g)
                    with sp.Fori(1, TURNS) as i:
                        load(i, g)

            @block.gpsimd
            def _(pool):
                nc.gpsimd.memset(zeros[:], 0.0).then_inc(zeroed, 1)
                nc.gpsimd.memset(none[:], 0.0).then_inc(none_set, 1)
                pool.wait_ge(none_set, 1)

                def split(i):
                    for s in range(2):
                        pool.wait_ge(w_loaded[s], i * 16 + 16)
                        if not isinstance(i, int):
                            pool.wait_ge(down_done, i * (2 * GCH) + (s - 1) * GCH)
                        nc.gpsimd.tensor_tensor(wh[:, s, :], wraw[:, s, :],
                                                none[:].broadcast_to([P, WCOL]), ALU.add).then_inc(w_half, 1)
                        pool.wait_ge(w_half, i * 2 + (s + 1))
                        nc.gpsimd.tensor_tensor(wl[:, s, :], wraw[:, s, 0:WBLK], wh[:, s, 0:WBLK].bitcast(F32),
                                                ALU.subtract).then_inc(w_split, 1)

                split(0)
                with pool.Fori(1, GROUPS * TURNS) as i:
                    split(i)

            @block.tensor
            def _(pe):
                pe.wait_ge(zeroed, 1)

                def hidden(bank, s, col, g, c, done):
                    tok = slice((g * GCH + c) * CHUNK, (g * GCH + c + 1) * CHUNK)
                    parts = [(w, a, k) for k in range(KD) for w, a in ((wh, xh), (wh, xl), (wl, xh))]
                    for m, (w, a, k) in enumerate(parts):
                        last = nc.tensor.matmul(bank[:], w[:, s, col + k * P:col + (k + 1) * P], a[:, k, tok],
                                                start=(m == 0), stop=(m == len(parts) - 1))
                    last.then_inc(done, 1)

                def down(st, count):
                    s, c = st // GCH, st % GCH
                    pe.wait_ge(lo_done, count)
                    for t in range(TPC):
                        tile = c * TPC + t
                        for a, w in ((hh, wh), (hh, wl), (hl, wh)):
                            last = nc.tensor.matmul(acc[tile // 2][:, tile % 2, :], a[:, st % 2, t * P:(t + 1) * P],
                                                    w[:, s, 2 * D:3 * D], start=False, stop=False,
                                                    skip_group_check=True)
                    last.then_inc(down_done, 1)

                def body(turn, g, routed, first):
                    for st in range(STEPS):
                        s, c = st // GCH, st % GCH
                        if c == 0:
                            pe.wait_ge(w_split, turn * 2 + (s + 1))
                        after(pe, silu_done, turn * STEPS + st)
                        hidden(pg, s, 0, g, c, gate_done)
                        after(pe, prod_done, turn * STEPS + st)
                        hidden(pu, s, D, g, c, up_done)
                        if routed:
                            after(pe, hid_done, turn * STEPS + st)
                            tok = slice((g * GCH + c) * CHUNK, (g * GCH + c + 1) * CHUNK)
                            nc.tensor.matmul(pc[:], wh[:, s, WBLK:WCOL], combT[:, tok], start=True,
                                             stop=True).then_inc(comb_done, 1)
                        if not (first and st == 0):
                            down((st - 1) % STEPS, turn * STEPS + st)

                def group(g):
                    if g:
                        pe.wait_ge(y_out, g * len(acc))
                    for a in acc:
                        nc.tensor.matmul(flat(a[:]), zeros[:, 0:P], zeros[:], start=True, stop=False,
                                         skip_group_check=True)

                group(0)
                for g in turns(pe, body):
                    down(STEPS - 1, (g + 1) * TURNS * STEPS)
                    if g + 1 < GROUPS:
                        group(g + 1)

            @block.scalar
            def _(act):
                def body(turn, g, routed, first):
                    for st in range(STEPS):
                        n = turn * STEPS + (st + 1)
                        act.wait_ge(gate_done, n)
                        nc.scalar.activation(gate[:, st % 2, :], pg[:], ACT.Silu).then_inc(silu_done, 1)
                        act.wait_ge(hid_done, n)
                        nc.scalar.activation(hh[:, st % 2, :], hid[:, st % 2, :], ACT.Copy).then_inc(hi_done, 1)

                for g in turns(act, body):
                    act.wait_ge(down_done, (g + 1) * TURNS * STEPS)
                    for n in range(0, len(acc), 2):
                        nc.scalar.activation(y[:, g * GT + 2 * n:g * GT + 2 * n + 2, :], acc[n][:],
                                             ACT.Copy).then_inc(y_out, 1)

            @block.vector
            def _(dve):
                def body(turn, g, routed, first):
                    for st in range(STEPS):
                        n = turn * STEPS + (st + 1)
                        dve.wait_ge(silu_done, n)
                        dve.wait_ge(up_done, n)
                        nc.vector.tensor_tensor(prod[:, st % 2, :], gate[:, st % 2, :], pu[:],
                                                ALU.mult).then_inc(prod_done, 1)
                        dve.wait_ge(prod_done, n)
                        if routed:
                            dve.wait_ge(comb_done, n - g * TURNS_S * STEPS)
                            ins_ = nc.vector.tensor_tensor(hid[:, st % 2, :], prod[:, st % 2, :], pc[:], ALU.mult)
                        else:
                            ins_ = nc.vector.tensor_copy(hid[:, st % 2, :], prod[:, st % 2, :])
                        ins_.then_inc(hid_done, 1)
                        dve.wait_ge(hi_done, n)
                        nc.vector.tensor_tensor(hl[:, st % 2, :], hid[:, st % 2, :],
                                                hh[:, st % 2, :].bitcast(F32), ALU.subtract).then_inc(lo_done, 1)

                for g in turns(dve, body):
                    dve.wait_ge(down_done, (g + 1) * TURNS * STEPS)
                    for n in range(1, len(acc), 2):
                        nc.vector.tensor_copy(y[:, g * GT + 2 * n:g * GT + 2 * n + 2, :],
                                              acc[n][:]).then_inc(y_out, 1)



TAPS = 4
CB_IN = 2 * NC + 1
PARTS = 3


def stage_ssm(chip, xh, xl, y, ident, ins):
    with ExitStack() as outer:
        sb, _ = chip.memory(outer)
        t = {
            "val": sb("val", [P, NT, DI]),
            "gateT": sb("gateT", [P, NC, TOK]),
        }
        with ExitStack() as mid:
            sb, _ = chip.memory(mid)
            t["ecum"] = sb("ecum", [P, NT, SH])
            t["erem"] = sb("erem", [P, NT, SH])
            t["cparts"] = sb("cparts", [PARTS * SH, TOK], BF16)
            stage_ssm_in(chip, xh, xl, t, ident, ins)
            stage_ssm_heads(chip, xh, xl, t, ins)
        stage_ssm_out(chip, t, y, ident, ins)


def stage_ssm_in(chip, xh, xl, t, ident, ins):
    nc = chip.nc
    val, gateT = t["val"], t["gateT"]
    with ExitStack() as ctx:
        sb, pb = chip.memory(ctx)
        z = sb("z", [SH, TOK])
        ld_tok = sb("ld_tok", [P, NT, SH])
        tri = sb("tri", [P, 2, P])
        chan = sb("chan", [P, NC, TAPS + 1])
        head = sb("head", [SH, 2])
        rate = sb("rate", [SH, 1])
        loaded = chip.sem("loaded")
        with ExitStack() as inner:
            sb, pb = chip.memory(inner)
            wraw = sb("wraw", [P, KD, CB_IN * P])
            wh = sb("wh", [P, KD, CB_IN * P], F32R)
            wl = sb("wl", [P, KD, CB_IN * P], F32R)
            pad = sb("pad", [P, 2, CHUNK // S, TAPS - 1 + S])
            conv = sb("conv", [P, 2, CHUNK // S, S])
            valT = sb("valT", [P, 2, CHUNK])
            pin = [pb(f"pin{n}", [P, CHUNK]) for n in range(3)]
            pv = [pb(f"pv{n}", [P, CHUNK]) for n in range(2)]
            raw_loaded, split_done = chip.sem("raw_loaded"), chip.sem("split_done")
            padded = chip.sem("padded")
            proj_done, taken = chip.sem("proj_done"), chip.sem("taken")
            conv_link, conv_done = chip.sem("conv_link"), chip.sem("conv_done")
            silu_done, val_turned, val_out = chip.sem("silu_done"), chip.sem("val_turned"), chip.sem("val_out")
            with nc.Block() as block:
                @block.sync
                def _(sp):
                    sp.dma_start(wraw[:], ins["w_in"]).then_inc(raw_loaded, 16)
                    for dst, src in ((tri, "tri"), (chan, "chan"), (head, "head")):
                        sp.dma_start(dst[:], ins[src]).then_inc(loaded, 16)

                @block.gpsimd
                def _(pool):
                    nc.gpsimd.memset(pad[:], 0.0).then_inc(padded, 1)

                @block.tensor
                def _(pe):
                    pe.wait_ge(split_done, 2)
                    parts = [(w, a, k) for k in range(KD) for w, a in ((wh, xh), (wh, xl), (wl, xh))]
                    def body(c):
                        for blk in range(CB_IN + 1):
                            if blk < CB_IN:
                                if blk < 3:
                                    after(pe, taken, c * CB_IN)
                                else:
                                    pe.wait_ge(taken, c * CB_IN + (blk - 2))
                                for m, (w, a, k) in enumerate(parts):
                                    last = nc.tensor.matmul(pin[blk % 3][:], w[:, k, blk * P:(blk + 1) * P],
                                                            a[:, k, bass.ts(c, CHUNK)],
                                                            start=(m == 0), stop=(m == len(parts) - 1))
                                last.then_inc(proj_done, 1)
                            if 2 <= blk < 2 + NC:
                                v = blk - 2
                                pe.wait_ge(silu_done, c * NC + (v + 1))
                                if v >= 2:
                                    pe.wait_ge(val_out, c * NC + (v - 1))
                                else:
                                    after(pe, val_out, c * NC)
                                for n in range(TPC):
                                    last = nc.tensor.transpose(pv[v % 2][:, n * P:(n + 1) * P],
                                                               valT[:, v % 2, n * P:(n + 1) * P], ident[:])
                                last.then_inc(val_turned, 1)

                    repeat(pe, NCH, body)

                @block.scalar
                def _(act):
                    act.wait_ge(loaded, 3 * 16)
                    act.wait_ge(padded, 1)
                    def body(c):
                        for blk in range(CB_IN):
                            act.wait_ge(proj_done, c * CB_IN + (blk + 1))
                            src = pin[blk % 3]
                            if blk < NC:
                                if blk >= 2:
                                    act.wait_ge(conv_done, c * NC + (blk - 1))
                                ins_ = nc.scalar.activation(pad[:, blk % 2, :, TAPS - 1:],
                                                            src[:].rearrange("p (b s) -> p b s", s=S), ACT.Copy)
                            elif blk < 2 * NC:
                                ins_ = nc.scalar.activation(gateT[:, blk - NC, bass.ts(c, CHUNK)], src[:], ACT.Silu)
                            else:
                                ins_ = nc.scalar.activation(z[:, bass.ts(c, CHUNK)], src[0:SH, :], ACT.Identity,
                                                            bias=head[:, 0:1])
                            ins_.then_inc(taken, 1)
                            if 1 <= blk < 1 + NC:
                                v = blk - 1
                                act.wait_ge(conv_done, c * NC + (v + 1))
                                if v >= 2:
                                    act.wait_ge(val_turned, c * NC + (v - 1))
                                nc.scalar.activation(valT[:, v % 2, :], conv[:, v % 2, :, :]
                                                     .rearrange("p b s -> p (b s)"), ACT.Silu).then_inc(silu_done, 1)

                    repeat(act, NCH, body)

                @block.vector
                def _(dve):
                    dve.wait_ge(raw_loaded, 16)
                    nc.vector.tensor_copy(flat(wh[:]), flat(wraw[:])).then_inc(split_done, 1)
                    dve.wait_ge(split_done, 1)
                    nc.vector.tensor_tensor(flat(wl[:]), flat(wraw[:]), flat(wh[:]).bitcast(F32),
                                            ALU.subtract).then_inc(split_done, 1)
                    dve.wait_ge(loaded, 3 * 16)
                    def body(c):
                        for blk in range(NC + 1):
                            if blk < NC:
                                dve.wait_ge(taken, c * CB_IN + (blk + 1))
                                if blk >= 2:
                                    dve.wait_ge(silu_done, c * NC + (blk - 1))
                                dst = conv[:, blk % 2, :, :]
                                nc.vector.tensor_scalar(dst, pad[:, blk % 2, :, TAPS - 1:TAPS - 1 + S],
                                                        chan[:, blk, TAPS - 1:TAPS], chan[:, blk, TAPS:TAPS + 1],
                                                        ALU.mult, ALU.add).then_inc(conv_link, 1)
                                for k in range(TAPS - 2, -1, -1):
                                    dve.wait_ge(conv_link, c * (NC * (TAPS - 1)) + (blk * (TAPS - 1) + TAPS - 1 - k))
                                    last = nc.vector.scalar_tensor_tensor(dst, pad[:, blk % 2, :, k:k + S],
                                                                          chan[:, blk, k:k + 1], dst,
                                                                          ALU.mult, ALU.add)
                                    last.then_inc(conv_link if k else conv_done, 1)
                            if blk >= 1:
                                v = blk - 1
                                dve.wait_ge(val_turned, c * NC + (v + 1))
                                nc.vector.tensor_copy(val[:, bass.ts(c, TPC), v * P:(v + 1) * P],
                                                      pv[v % 2][:].rearrange("p (t n) -> p t n", n=P)
                                                      ).then_inc(val_out, 1)

                    repeat(dve, NCH, body)

        with ExitStack() as inner:
            sb, pb = chip.memory(inner)
            soft = sb("soft", [SH, TOK])
            cum = sb("cum", [SH, CHUNK])
            part = sb("part", [SH, CHUNK], BF16)
            pt = pb("pt", [P, NT, SH])
            pcum, prem = pb("pcum", [P, NT * SH]), pb("prem", [P, NT * SH])
            pcT = [pb(f"pcT{n}", [SH, CHUNK]) for n in range(NCH)]
            act_link, chain = chip.sem("act_link"), chip.sem("decay_chain")
            soft_done, ld_done, ld_turned = chip.sem("soft_done"), chip.sem("ld_done"), chip.sem("ld_turned")
            ld_copied, sums_done, exps_done = chip.sem("ld_copied"), chip.sem("sums_done"), chip.sem("exps_done")
            with nc.Block() as block:
                @block.scalar
                def _(act):
                    link = linker(act, act_link)
                    link(nc.scalar.activation(rate[:], head[:, 1:2], ACT.Exp))
                    link(nc.scalar.activation(soft[:], z[:], ACT.Abs))
                    link(nc.scalar.activation(soft[:], soft[:], ACT.Exp, scale=-1.0))
                    link(nc.scalar.activation(soft[:], soft[:], ACT.Ln, bias=1.0))
                    nc.scalar.sem_inc(soft_done, 1)
                    act.wait_ge(sums_done, 1)
                    nc.scalar.activation(flat(t["ecum"][:]), pcum[:], ACT.Exp)
                    nc.scalar.activation(flat(t["erem"][:]), prem[:], ACT.Exp)

                @block.vector
                def _(dve):
                    link = linker(dve, chain)
                    dve.wait_ge(soft_done, 1)
                    link(nc.vector.scalar_tensor_tensor(z[:], z[:], 0.0, soft[:], ALU.max, ALU.add))
                    nc.vector.tensor_scalar(z[:], z[:], rate[:, 0:1], -1.0, ALU.mult, ALU.mult).then_inc(ld_done, 1)
                    dve.wait_ge(ld_turned, 1)
                    nc.vector.tensor_copy(ld_tok[:], pt[:]).then_inc(ld_copied, 1)
                    dve.wait_ge(sums_done, 2)
                    for c in range(NCH):
                        cols = slice(c * CHUNK, (c + 1) * CHUNK)
                        link(nc.vector.tensor_copy(t["cparts"][0:SH, cols], pcT[c][:]))
                        link(nc.vector.tensor_tensor(cum[:], pcT[c][:], t["cparts"][0:SH, cols], ALU.subtract))
                        link(nc.vector.tensor_copy(part[:], cum[:]))
                        nc.vector.tensor_copy(t["cparts"][SH:2 * SH, cols], part[:])
                        link(nc.vector.tensor_tensor(cum[:], cum[:], part[:], ALU.subtract))
                        link(nc.vector.tensor_copy(t["cparts"][2 * SH:3 * SH, cols], cum[:]))

                @block.tensor
                def _(pe):
                    pe.wait_ge(ld_done, 1)
                    for n in range(NT):
                        last = nc.tensor.transpose(pt[:, n, :], z[:, n * P:(n + 1) * P], ident[0:SH, 0:SH])
                    last.then_inc(ld_turned, 1)
                    pe.wait_ge(ld_copied, 1)
                    nc.tensor.matmul(pcum[:], tri[:, 0, :], flat(ld_tok[:]), start=True, stop=True)
                    nc.tensor.matmul(prem[:], tri[:, 1, :], flat(ld_tok[:]), start=True,
                                     stop=True).then_inc(sums_done, 1)
                    for n in range(NT):
                        last = nc.tensor.matmul(pcT[n // TPC][:, (n % TPC) * P:(n % TPC + 1) * P], ld_tok[:, n, :],
                                                tri[:, 0, :], start=True, stop=True)
                    last.then_inc(sums_done, 1)


def stage_ssm_heads(chip, xh, xl, t, ins):
    nc = chip.nc
    val, ecum, erem, cparts = t["val"], t["ecum"], t["erem"], t["cparts"]
    WCOL = 2 * KD * P
    BPC = CHUNK // S
    STEPS = 2 * NCH
    TURNS = SH // 2
    ROWS = PARTS * SH
    with ExitStack() as ctx:
        sb, pb = chip.memory(ctx)
        wraw = sb("wraw", [P, 2, WCOL])
        wh = sb("wh", [P, 2, WCOL], F32R)
        wl = sb("wl", [P, 2, WCOL], F32R)
        sel = sb("sel", [ROWS, 2, SH * P], BF16)
        identb = sb("identb", [P, P], BF16)
        mask = sb("mask", [P, TPC * P], BF16)
        skip = sb("skip", [P, DI])
        bT = sb("bT", [P, 2, CHUNK])
        cT = sb("cT", [P, 2, CHUNK])
        decay = sb("decay", [P, 2, CHUNK])
        mixT = sb("mixT", [P, 2, TPC, P])
        cross = sb("cross", [P, 2, BPC, P])
        vdec = sb("vdec", [P, 2, B, SHD])
        vskip = sb("vskip", [P, 2, NT, SHD])
        late = sb("late", [P, B, SHD])
        none = sb("none", [P, 1])
        pbT, pcT, pdec = pb("pbT", [P, CHUNK]), pb("pcT", [P, CHUNK]), pb("pdec", [P, CHUNK])
        pcb = [pb(f"pcb{n}", [P, 3, P]) for n in range(BPC)]
        py = [pb(f"py{n}", [P, NT + B, SHD]) for n in range(2)]
        loaded = chip.sem("loaded")
        w_loaded = [chip.sem("w_loaded") for _ in range(2)]
        w_half, w_split = chip.sem("w_half"), chip.sem("w_split")
        b_done, c_done, dec_done = chip.sem("b_done"), chip.sem("c_done"), chip.sem("dec_done")
        b_out, c_out, dec_out = chip.sem("b_out"), chip.sem("c_out"), chip.sem("dec_out")
        cb_done, mix_out, cross_out = chip.sem("cb_done"), chip.sem("mix_out"), chip.sem("cross_out")
        y_done, late_out, y_out = chip.sem("y_done"), chip.sem("late_out"), chip.sem("y_out")
        v_ready, none_set = chip.sem("v_ready"), chip.sem("none_set")

        def turns(eng, body):
            body(0, True)
            with eng.Fori(1, TURNS) as i:
                body(i, False)

        def head_cols(turn, hp):
            return bass.ds(turn * (2 * SHD) + hp * SHD, SHD)

        with nc.Block() as block:
            @block.sync
            def _(sp):
                for dst, src in ((sel, "head_rows"), (identb, "identb"), (mask, "mask_turned"), (skip, "skip")):
                    sp.dma_start(dst[:], ins[src]).then_inc(loaded, 16)

                def body(turn, first):
                    for s in range(2):
                        if not first:
                            sp.wait_ge(w_split, turn * 2 + (s - 1))
                        sp.dma_start(wraw[:, s, :], ins["w_bc"][bass.ds(turn * 2 + s, 1), :, :]
                                     .rearrange("a p n -> p (a n)")).then_inc(w_loaded[s], 16)

                turns(sp, body)

            @block.gpsimd
            def _(pool):
                nc.gpsimd.memset(none[:], 0.0).then_inc(none_set, 1)
                pool.wait_ge(none_set, 1)
                pool.wait_ge(loaded, 4 * 16)

                def body(turn, first):
                    for s in range(2):
                        pool.wait_ge(w_loaded[s], turn * 16 + 16)
                        if not first:
                            pool.wait_ge(c_done, turn * STEPS + (s - 1) * NCH)
                        nc.gpsimd.tensor_tensor(wh[:, s, :], wraw[:, s, :],
                                                none[:].broadcast_to([P, WCOL]), ALU.add).then_inc(w_half, 1)
                        pool.wait_ge(w_half, turn * 2 + (s + 1))
                        nc.gpsimd.tensor_tensor(wl[:, s, :], wraw[:, s, :], wh[:, s, :].bitcast(F32),
                                                ALU.subtract).then_inc(w_split, 1)
                        if not first:
                            pool.wait_ge(y_out, turn * 2 + (s - 1))
                        cols = head_cols(turn, s)
                        head = bass.ds(turn * 2 + s, 1)
                        nc.gpsimd.tensor_tensor(vdec[:, s, :, :], val[:, 0:NT:2, cols],
                                                erem[:, 0:NT:2, head].broadcast_to([P, B, SHD]), ALU.mult)
                        nc.gpsimd.tensor_tensor(vskip[:, s, :, :], val[:, :, cols],
                                                skip[:, cols].unsqueeze(1).broadcast_to([P, NT, SHD]),
                                                ALU.mult).then_inc(v_ready, 1)

                turns(pool, body)

            @block.tensor
            def _(pe):
                pe.wait_ge(loaded, 4 * 16)

                def project(bank, s, what, c, done):
                    parts = [(w, a, k) for k in range(KD) for w, a in ((wh, xh), (wh, xl), (wl, xh))]
                    for m, (w, a, k) in enumerate(parts):
                        col = (what * KD + k) * P
                        last = nc.tensor.matmul(bank[:], w[:, s, col:col + P], a[:, k, c * CHUNK:(c + 1) * CHUNK],
                                                start=(m == 0), stop=(m == len(parts) - 1))
                    last.then_inc(done, 1)

                def decays(turn, s, c):
                    head = bass.ds(turn * (2 * P) + s * P, P)
                    nc.tensor.matmul(pdec[:], sel[:, 0, head], cparts[:, c * CHUNK:(c + 1) * CHUNK],
                                     start=True, stop=False, skip_group_check=True)
                    for n in range(TPC):
                        nc.tensor.matmul(pdec[:, n * P:(n + 1) * P],
                                         cparts[:, c * CHUNK + n * P:c * CHUNK + (n + 1) * P], sel[:, 1, head],
                                         start=False, stop=False, skip_group_check=True)
                    nc.tensor.matmul(pdec[:], identb[:], mask[:], start=False, stop=True,
                                     skip_group_check=True).then_inc(dec_done, 1)

                def products(st, count):
                    pe.wait_ge(b_out, count)
                    pe.wait_ge(c_out, count)
                    for q in range(BPC):
                        o = q * S
                        nc.tensor.matmul(pcb[q][:, 0:2, :], bT[:, st % 2, o:o + P], cT[:, st % 2, o:o + S],
                                         start=True, stop=True)
                        last = nc.tensor.matmul(pcb[q][:, 2, :], bT[:, st % 2, o + P:o + S],
                                                cT[:, st % 2, o + P:o + S], start=True, stop=True)
                    last.then_inc(cb_done, 1)

                def outputs(turn, st, count):
                    s, c = st // NCH, st % NCH
                    pe.wait_ge(mix_out, count)
                    pe.wait_ge(cross_out, count)
                    cols = head_cols(turn, s)
                    for n in range(TPC):
                        tile = c * TPC + n
                        nc.tensor.matmul(py[s][:, tile, :], mixT[:, st % 2, n, :], val[:, tile, cols],
                                         start=True, stop=True)
                    for q in range(BPC):
                        seq = c * BPC + q
                        last = nc.tensor.matmul(py[s][:, NT + seq, :], cross[:, st % 2, q, :], vdec[:, s, seq, :],
                                                start=True, stop=True)
                    last.then_inc(y_done, 1)

                def body(turn, first):
                    for st in range(STEPS):
                        s, c = st // NCH, st % NCH
                        if c == 0:
                            pe.wait_ge(w_split, turn * 2 + (s + 1))
                        after(pe, b_out, turn * STEPS + st)
                        project(pbT, s, 0, c, b_done)
                        after(pe, dec_out, turn * STEPS + st)
                        decays(turn, s, c)
                        after(pe, c_out, turn * STEPS + st)
                        project(pcT, s, 1, c, c_done)
                        if not (first and st < 2):
                            pe.wait_ge(mix_out, turn * STEPS + (st - 1))
                            pe.wait_ge(cross_out, turn * STEPS + (st - 1))
                        if not (first and st == 0):
                            products((st - 1) % STEPS, turn * STEPS + st)
                        if not (first and st < 2):
                            if c == 2:
                                pe.wait_ge(v_ready, turn * 2 + (s + 1))
                                if not first:
                                    pe.wait_ge(y_out, turn * 2 + (s - 1))
                            if st >= 2:
                                outputs(turn, st - 2, turn * STEPS + (st - 1))
                            else:
                                outputs(turn - 1, st - 2 + STEPS, turn * STEPS + (st - 1))

                turns(pe, body)
                end = TURNS * STEPS
                pe.wait_ge(mix_out, end - 1)
                pe.wait_ge(cross_out, end - 1)
                products(STEPS - 1, end)
                outputs(TURNS - 1, STEPS - 2, end - 1)
                outputs(TURNS - 1, STEPS - 1, end)

            @block.scalar
            def _(act):
                def cross_copy(st, count):
                    act.wait_ge(cb_done, count)
                    for q in range(BPC):
                        last = nc.scalar.activation(cross[:, st % 2, q, :], pcb[q][:, 1, :], ACT.Copy)
                    last.then_inc(cross_out, 1)

                def body(turn, first):
                    for st in range(STEPS):
                        n = turn * STEPS + st
                        act.wait_ge(b_done, n + 1)
                        if not (first and st < 2):
                            act.wait_ge(cb_done, turn * STEPS + (st - 1))
                        nc.scalar.activation(bT[:, st % 2, :], pbT[:], ACT.Copy).then_inc(b_out, 1)
                        act.wait_ge(dec_done, n + 1)
                        if not (first and st < 2):
                            act.wait_ge(mix_out, turn * STEPS + (st - 1))
                        nc.scalar.activation(decay[:, st % 2, :], pdec[:], ACT.Exp).then_inc(dec_out, 1)
                        if not (first and st == 0):
                            if not (first and st < 3):
                                act.wait_ge(y_done, turn * STEPS + (st - 2))
                            cross_copy((st - 1) % STEPS, turn * STEPS + st)

                turns(act, body)
                act.wait_ge(y_done, TURNS * STEPS - 2)
                cross_copy(STEPS - 1, TURNS * STEPS)

            @block.vector
            def _(dve):
                def mix(st, count):
                    dve.wait_ge(cross_out, count)
                    dve.wait_ge(dec_out, count)
                    for q in range(BPC):
                        last = nc.vector.tensor_tensor(
                            mixT[:, st % 2, 2 * q:2 * q + 2, :], pcb[q][:, 0:3:2, :],
                            decay[:, st % 2, q * S:(q + 1) * S].rearrange("p (n l) -> p n l", l=P), ALU.mult)
                    last.then_inc(mix_out, 1)

                def take(turn, s, heads):
                    dve.wait_ge(y_done, heads * NCH)
                    dve.wait_ge(v_ready, heads)
                    cols = head_cols(turn, s)
                    head = bass.ds(turn * 2 + s, 1)
                    nc.vector.tensor_tensor(late[:], py[s][:, NT:, :], ecum[:, 1:NT:2, head]
                                            .broadcast_to([P, B, SHD]), ALU.mult)
                    nc.vector.tensor_tensor(val[:, :, cols], py[s][:, 0:NT, :], vskip[:, s, :, :],
                                            ALU.add).then_inc(late_out, 1)
                    dve.wait_ge(late_out, heads)
                    nc.vector.tensor_tensor(val[:, 1:NT:2, cols], val[:, 1:NT:2, cols], late[:],
                                            ALU.add).then_inc(y_out, 1)

                def body(turn, first):
                    for st in range(STEPS):
                        s, c = st // NCH, st % NCH
                        dve.wait_ge(c_done, turn * STEPS + (st + 1))
                        if not (first and st < 2):
                            dve.wait_ge(cb_done, turn * STEPS + (st - 1))
                        nc.vector.tensor_copy(cT[:, st % 2, :], pcT[:]).then_inc(c_out, 1)
                        if not (first and st == 0):
                            if not (first and st < 3):
                                dve.wait_ge(y_done, turn * STEPS + (st - 2))
                            mix((st - 1) % STEPS, turn * STEPS + st)
                        if c == 2 and not (first and s == 0):
                            if s == 1:
                                take(turn, 0, turn * 2 + 1)
                            else:
                                take(turn - 1, 1, turn * 2)

                turns(dve, body)
                end = TURNS * STEPS
                dve.wait_ge(y_done, end - 2)
                mix(STEPS - 1, end)
                take(TURNS - 1, 1, SH)


def stage_ssm_out(chip, t, y, ident, ins):
    nc = chip.nc
    val, gateT = t["val"], t["gateT"]
    with ExitStack() as ctx:
        sb, pb = chip.memory(ctx)
        wout = sb("wout", [P, NC, D])
        staged = sb("staged", [P, 2, 2, DI])
        zT = sb("zT", [P, 2, NC, S])
        pt = [pb(f"pt{n}", [P, 2, S]) for n in range(4)]
        po = [pb(f"po{n}", [P, 2, D]) for n in range(2)]
        loaded, stage_done, turned = chip.sem("loaded"), chip.sem("stage_done"), chip.sem("turned")
        gated, projected, y_out = chip.sem("gated"), chip.sem("projected"), chip.sem("y_out")
        with nc.Block() as block:
            @block.sync
            def _(sp):
                sp.dma_start(wout[:], ins["w_out"]).then_inc(loaded, 16)

            @block.gpsimd
            def _(pool):
                def body(i):
                    after(pool, turned, i * 2)
                    for s in range(2):
                        nc.gpsimd.tensor_copy(staged[:, s, :, :],
                                              val[:, bass.ds(i * 4 + 2 * s, 2), :]).then_inc(stage_done, 1)

                repeat(pool, B // 2, body)

            @block.tensor
            def _(pe):
                pe.wait_ge(loaded, 16)
                def body(i):
                    for s in range(2):
                        pe.wait_ge(stage_done, i * 2 + (s + 1))
                        after(pe, gated, i * 2)
                        for blk in range(NC):
                            for n in range(2):
                                last = nc.tensor.transpose(pt[2 * s + blk // 2][:, blk % 2, n * P:(n + 1) * P],
                                                           staged[:, s, n, blk * P:(blk + 1) * P], ident[:])
                        last.then_inc(turned, 1)
                    for s in range(2):
                        pe.wait_ge(gated, i * 2 + (s + 1))
                        after(pe, y_out, i * 2)
                        for n in range(2):
                            for blk in range(NC):
                                last = nc.tensor.matmul(po[s][:, n, :], zT[:, s, blk, n * P:(n + 1) * P],
                                                        wout[:, blk, :], start=(blk == 0), stop=(blk == NC - 1))
                        last.then_inc(projected, 1)

                repeat(pe, B // 2, body)

            @block.scalar
            def _(act):
                def body(i):
                    for s in range(2):
                        act.wait_ge(projected, i * 2 + (s + 1))
                        nc.scalar.activation(y[:, bass.ds(i * 4 + 2 * s, 2), :], po[s][:],
                                             ACT.Copy).then_inc(y_out, 1)

                repeat(act, B // 2, body)

            @block.vector
            def _(dve):
                def body(i):
                    for s in range(2):
                        dve.wait_ge(turned, i * 2 + (s + 1))
                        after(dve, projected, i * 2)
                        for half in range(2):
                            blks = slice(2 * half, 2 * half + 2)
                            last = nc.vector.tensor_tensor(zT[:, s, blks, :], pt[2 * s + half][:],
                                                           gateT[:, blks, bass.ds(i * (2 * S) + s * S, S)], ALU.mult)
                        last.then_inc(gated, 1)

                repeat(dve, B // 2, body)



def stage_ffn(chip, xh, y, ins):
    nc = chip.nc
    WCOL = 2 * D
    with ExitStack() as ctx:
        sb, pb = chip.memory(ctx)
        wraw = sb("wraw", [P, NFH, WCOL])
        wh = sb("wh", [P, NFH, WCOL], F32R)
        wl = sb("wl", [P, NFH, WCOL], F32R)
        bias0 = sb("bias0", [P, NFH])
        bias1 = sb("bias1", [P, D])
        act16 = sb("act16", [P, 2, CHUNK], F16)
        hid = sb("hid", [P, 2, CHUNK], F32R)
        y16 = sb("y16", [P, TPC, D], F16)
        ph = [pb(f"ph{n}", [P, CHUNK]) for n in range(2)]
        acc = [pb(f"acc{n}", [P, D]) for n in range(TPC)]
        raw_loaded = chip.sem("raw_loaded")
        loaded, split_half, split_done = chip.sem("loaded"), chip.sem("split_half"), chip.sem("split_done")
        up_done, gelu_done, hid_done = chip.sem("up_done"), chip.sem("gelu_done"), chip.sem("hid_done")
        down_done, y_half, y_out = chip.sem("down_done"), chip.sem("y_half"), chip.sem("y_out")
        with nc.Block() as block:
            @block.sync
            def _(sp):
                sp.dma_start(wraw[:], ins["ffn_w"]).then_inc(raw_loaded, 16)
                sp.dma_start(bias0[:], ins["ffn_b0"]).then_inc(loaded, 16)
                sp.dma_start(bias1[:], ins["ffn_b1"]).then_inc(loaded, 16)

            @block.tensor
            def _(pe):
                pe.wait_ge(split_done, 2)

                def up(c, n):
                    parts = [(w, k) for k in range(KD) for w in (wh, wl)]
                    for m, (w, k) in enumerate(parts):
                        last = nc.tensor.matmul(ph[n % 2][:], w[:, n, k * P:(k + 1) * P],
                                                xh[:, k, bass.ts(c, CHUNK)], start=(m == 0), stop=(m == len(parts) - 1))
                    last.then_inc(up_done, 1)

                def down(n):
                    for t in range(TPC):
                        for m, w in enumerate((wh, wl)):
                            last = nc.tensor.matmul(acc[t][:], hid[:, n % 2, t * P:(t + 1) * P], w[:, n, D:2 * D],
                                                    start=(n == 0 and m == 0), stop=(n == NFH - 1 and m == 1))
                    last.then_inc(down_done, 1)

                def body(c):
                    for n in range(NFH + 1):
                        if n < NFH:
                            after(pe, gelu_done, c * NFH + max(n - 1, 0))
                            up(c, n)
                        if n == 1:
                            after(pe, y_half, c)
                        if n >= 1:
                            pe.wait_ge(hid_done, c * NFH + n)
                            down(n - 1)

                repeat(pe, NCH, body)

            @block.scalar
            def _(act):
                act.wait_ge(loaded, 32)
                def body(c):
                    for n in range(NFH):
                        act.wait_ge(up_done, c * NFH + (n + 1))
                        after(act, hid_done, c * NFH + max(n - 1, 0))
                        nc.scalar.activation(act16[:, n % 2, :], ph[n % 2][:], ACT.Gelu,
                                             bias=bias0[:, n:n + 1]).then_inc(gelu_done, 1)

                repeat(act, NCH, body)

            @block.vector
            def _(dve):
                dve.wait_ge(raw_loaded, 16)
                nc.vector.tensor_copy(flat(wh[:]), flat(wraw[:])).then_inc(split_half, 1)
                dve.wait_ge(split_half, 1)
                nc.vector.tensor_tensor(flat(wl[:]), flat(wraw[:]), flat(wh[:]).bitcast(F32),
                                        ALU.subtract).then_inc(split_done, 2)
                dve.wait_ge(loaded, 32)
                def body(c):
                    for n in range(NFH):
                        dve.wait_ge(gelu_done, c * NFH + (n + 1))
                        after(dve, down_done, c * NFH + max(n - 1, 0))
                        nc.vector.tensor_copy(hid[:, n % 2, :], act16[:, n % 2, :]).then_inc(hid_done, 1)
                    dve.wait_ge(down_done, c * NFH + NFH)
                    for t in range(TPC):
                        last = nc.vector.tensor_tensor(y16[:, t, :], acc[t][:], bias1[:], ALU.add)
                    last.then_inc(y_half, 1)
                    dve.wait_ge(y_half, c + 1)
                    nc.vector.tensor_copy(y[:, bass.ts(c, TPC), :], y16[:]).then_inc(y_out, 1)

                repeat(dve, NCH, body)


def program(nc, io):
    with ExitStack() as sems, ExitStack() as mem:
        chip = Chip(nc, sems)
        x = mem.enter_context(nc.sbuf_tensor("x", [P, NT, D], F32))
        y = mem.enter_context(nc.sbuf_tensor("y", [P, NT, D], F32))
        xh = mem.enter_context(nc.sbuf_tensor("xh", [P, KD, TOK], F32R))
        xl = mem.enter_context(nc.sbuf_tensor("xl", [P, KD, TOK], F32R))
        ident = mem.enter_context(nc.sbuf_tensor("ident", [P, P], F32))
        x_loaded = chip.sem("x_loaded")
        with nc.Block() as block:
            @block.sync
            def _(sp):
                sp.dma_start(x[:], io["x"]).then_inc(x_loaded, 16)
                sp.dma_start(ident[:], io["ident"]).then_inc(x_loaded, 16)
                sp.wait_ge(x_loaded, 32)
        stage_norm(chip, x, y, xh, xl, ident, False, True)
        stage_attention(chip, xh, xl, y, ident, io)
        stage_norm(chip, x, y, xh, xl, ident, True, True)
        stage_moe(chip, xh, xl, y, ident, io)
        stage_norm(chip, x, y, xh, xl, ident, True, True)
        stage_ssm(chip, xh, xl, y, ident, io)
        stage_norm(chip, x, y, xh, xl, ident, True, True, half=True)
        stage_ffn(chip, xh, y, io)
        stage_norm(chip, x, y, xh, xl, ident, True, False, out=io["out"])



def slopes(n):
    start = 2.0 ** (-8.0 / n)
    return [start ** (i + 1) for i in range(n)]


def layouts(a):
    import numpy as np

    def bcast(v):
        return np.broadcast_to(v.reshape(1, -1), (P, v.size)).copy()

    out = {}
    out["x"] = a["L0_attn_hidden_states"].reshape(NT, P, D).transpose(1, 0, 2)
    w, bias = a["L0_attn_w_qkv"], a["L0_attn_b_qkv"]
    wqkv = np.zeros((P, KD, 2 * NG * P + D), np.float32)
    bqk = np.zeros((P, 2 * NG), np.float32)
    for part in range(2):
        cols = w[:, part * D:(part + 1) * D].reshape(KD, P, NG, HPG, HD).transpose(1, 0, 2, 3, 4)
        dst = wqkv[:, :, part * NG * P:(part + 1) * NG * P].reshape(P, KD, NG, HPG, HROW)
        dst[..., :HD] = cols
        wqkv[:, :, part * NG * P:(part + 1) * NG * P] = dst.reshape(P, KD, NG * P)
        b4 = bqk[:, part * NG:(part + 1) * NG].reshape(HPG, HROW, NG).copy()
        b4[:, :HD] = bias[part * D:(part + 1) * D].reshape(NG, HPG, HD).transpose(1, 2, 0)
        if part == 0:
            b4[:, HD] = np.array([s * HD for s in slopes(NH)], np.float32).reshape(NG, HPG).T
        bqk[:, part * NG:(part + 1) * NG] = b4.reshape(P, NG)
    wqkv[:, :, 2 * NG * P:] = w[:, 2 * D:].reshape(KD, P, D).transpose(1, 0, 2)
    out["wqkv"], out["bqk"] = wqkv, bqk
    out["bv"] = bcast(bias[2 * D:])
    out["wproj"] = a["L0_attn_w_proj"].reshape(KD, P, D).transpose(1, 0, 2)
    out["bproj"] = bcast(a["L0_attn_b_proj"])
    ramp = np.zeros((HPG, HROW, S), np.float32)
    ramp[:, HD] = np.arange(S, dtype=np.float32)
    out["ramp"] = ramp.reshape(P, S)
    low = np.tril(np.ones((P, P), bool))
    out["ident"] = np.eye(P, dtype=np.float32)
    out["identb"] = np.eye(P).astype(np.dtype("bfloat16"))
    out["causal_add"] = np.where(low, 0.0, -BIG).astype(np.dtype("bfloat16"))

    out["router_w"] = a["L0_ffn_router_w"].reshape(KD, P, NE).transpose(1, 0, 2)
    out["router_b"] = bcast(a["L0_ffn_router_bias"])
    select = np.zeros((ROUTED + SHARED, 2, NE, P // FE, FE), np.float32)
    for j in range(ROUTED):
        for n in range(P // FE):
            select[j, :, j * (P // FE) + n, n, :] = 1.0
    cols = []
    for routed, shared in (("wg", "swg"), ("wu", "swu")):
        r = a["L0_ffn_" + routed].reshape(ROUTED, P // FE, KD, P, FE).transpose(0, 3, 2, 1, 4)
        sh = a["L0_ffn_" + shared].reshape(2, KD, P, SHARED // 2, P).transpose(0, 3, 2, 1, 4)
        cols.append(np.concatenate([r.reshape(ROUTED, P, D), sh.reshape(SHARED, P, D)]))
    cols.append(np.concatenate([a["L0_ffn_wd"].reshape(ROUTED, P, D), a["L0_ffn_swd"].reshape(SHARED, P, D)]))
    cols.append(select.reshape(ROUTED + SHARED, P, P))
    out["experts"] = np.concatenate(cols, axis=2)
    w_in = a["L1_attn_W_in"].T
    nbc = SH * SN
    edge = np.zeros((D, CB_IN * P), np.float32)
    edge[:, :2 * DI] = w_in[:, :2 * DI]
    edge[:, 2 * DI:2 * DI + SH] = w_in[:, 2 * DI + 2 * nbc:]
    out["w_in"] = edge.reshape(KD, P, CB_IN * P).transpose(1, 0, 2)
    bc = w_in[:, 2 * DI:2 * DI + 2 * nbc].reshape(KD, P, 2, SH, SN)
    out["w_bc"] = bc.transpose(3, 1, 2, 0, 4).reshape(SH, P, 2 * KD * P)
    chan = np.concatenate([a["L1_attn_conv_w"].reshape(DI, TAPS), a["L1_attn_conv_b"].reshape(DI, 1)], axis=1)
    out["chan"] = chan.reshape(NC, P, TAPS + 1).transpose(1, 0, 2)
    out["head"] = np.stack([a["L1_attn_dt_bias"], a["L1_attn_A_log"]], axis=1)
    out["tri"] = np.stack([low.T, low & ~np.eye(P, dtype=bool)], axis=1).astype(np.float32)
    rows = np.zeros((PARTS, SH, 2, SH, P), np.float32)
    for h in range(SH):
        rows[:, h, 0, h], rows[:, h, 1, h] = 1.0, -1.0
    out["head_rows"] = rows.reshape(PARTS * SH, 2, SH * P).astype(np.dtype("bfloat16"))
    out["mask_turned"] = np.tile(np.where(low.T, 0.0, -BIG), (1, TPC)).astype(np.dtype("bfloat16"))
    out["skip"] = bcast(a["L1_attn_D_param"])
    out["w_out"] = a["L1_attn_W_out"].T.reshape(NC, P, D).transpose(1, 0, 2)

    w0 = a["L1_ffn_W0"].T.reshape(KD, P, NFH, P).transpose(1, 2, 0, 3).reshape(P, NFH, D)
    w1 = a["L1_ffn_W1"].T.reshape(NFH, P, D).transpose(1, 0, 2)
    out["ffn_w"] = np.concatenate([w0, w1], axis=2)
    out["ffn_b0"] = a["L1_ffn_bias0"].reshape(NFH, P).T
    out["ffn_b1"] = bcast(a["L1_ffn_bias1"])
    return {k: np.ascontiguousarray(v) for k, v in out.items()}


def kernel(**inputs):
    import concourse.bacc as bacc
    import numpy as np
    from concourse.bass_utils import run_bass_kernel_spmd

    arrays = layouts({k: np.asarray(v) for k, v in inputs.items()})
    nc = bacc.Bacc("TRN2", target_bir_lowering=False, num_devices=1)
    io = {}
    for name, v in arrays.items():
        io[name] = nc.dram_tensor(f"in_{name}", v.shape, mybir.dt.from_np(v.dtype), kind="ExternalInput").ap()
    io["out"] = nc.dram_tensor("result", (P, NT, D), mybir.dt.from_np(np.dtype("float32")),
                               kind="ExternalOutput").ap()
    program(nc, io)
    r = run_bass_kernel_spmd(nc, [{f"in_{k}": v for k, v in arrays.items()}], core_ids=[0])
    got = np.asarray(r.results[0]["result"])
    return got.reshape(P, NT, D).transpose(1, 0, 2).reshape(B, S, D)
```

```python
from contextlib import ExitStack

import concourse.bass as bass
from concourse import mybir

F32 = mybir.dt.float32
F32R = mybir.dt.float32r
BF16 = mybir.dt.bfloat16
F16 = mybir.dt.float16
ALU = mybir.AluOpType
ACT = mybir.ActivationFunctionType
AX = mybir.AxisListType

P = 128
D = 256
KD = D // P
B, S = 8, 256
NT = B * S // P
TOK = B * S
EPS = 1e-5

NH, HD = 16, 16

NE, FE, TOPK = 64, 64, 4
ROUTED = NE * FE // P
SHARED = 4
WBLK = 3 * D
BIG = 3.0e38

SH, SHD, SN = 32, 16, 128
DI = SH * SHD
NC = DI // P
CHUNK = 512
NCH = TOK // CHUNK
TPC = CHUNK // P

FH = 1024
NFH = FH // P


class Chip:

    def __init__(self, nc, sems):
        self.nc, self.sems, self.count = nc, sems, 0

    def sem(self, name):
        self.count += 1
        return self.sems.enter_context(self.nc.semaphore(f"{name}_{self.count}"))

    def memory(self, ctx):
        def sb(name, shape, dt=F32):
            self.count += 1
            return ctx.enter_context(self.nc.sbuf_tensor(f"{name}_{self.count}", shape, dt))

        def pb(name, shape):
            self.count += 1
            return ctx.enter_context(self.nc.psum_tensor(f"{name}_{self.count}", shape, F32))

        return sb, pb


def linker(eng, sem):
    n = [0]

    def link(ins):
        n[0] += 1
        ins.then_inc(sem, 1)
        eng.wait_ge(sem, n[0])

    return link


def repeat(eng, times, body):
    body(0)
    with eng.Fori(1, times) as i:
        body(i)


def after(eng, sem, value):
    if not isinstance(value, int) or value > 0:
        eng.wait_ge(sem, value)


def flat(ap):
    return ap.rearrange("p a b -> p (a b)")



NORM_GROUPS = 4
NORM_TILES = NT // NORM_GROUPS
NORM_SEQS = B // NORM_GROUPS


def stage_norm(chip, x, y, xh, xl, ident, add_y, make_norm, half=False, x_loaded=None, out=None):
    nc = chip.nc
    with ExitStack() as ctx:
        sb, pb = chip.memory(ctx)

        stats = sb("stats", [P, NT, 6])
        small = sb("small", [P, 6, NT])
        power = sb("power", [P, NT])
        negmean, var, rstd, shift = (sb(n, [P, 2, NT]) for n in ("negmean", "var", "rstd", "shift"))
        xn = sb("xn", [P, 2, 2, D])
        xn16 = sb("xn16", [P, 2, 2, D], F16)
        turned = [pb(f"turned{n}", [P, KD, S]) for n in range(2)]
        chain = chip.sem("norm_chain")
        pool_link = chip.sem("pool_link")
        var_ready = chip.sem("var_ready")
        rstd_ready = chip.sem("rstd_ready")
        if add_y:
            y_scaled = chip.sem("y_scaled")
        if not make_norm:
            x_final = chip.sem("x_final")
            stored = chip.sem("stored")
        if make_norm:
            xn_ready = chip.sem("xn_ready")
            xn_turned = chip.sem("xn_turned")
            hi_ready = chip.sem("hi_ready")
            lo_ready = None if half else chip.sem("lo_ready")
            xn_rounded = chip.sem("xn_rounded") if half else None
        norms = [n for n in range(2) if (add_y, make_norm)[n]]
        x_base = NORM_GROUPS if add_y else 0

        def tiles(g):
            return slice(g * NORM_TILES, (g + 1) * NORM_TILES)

        with nc.Block() as block:
            @block.gpsimd
            def _(pool):
                link = linker(pool, pool_link)
                link(nc.gpsimd.memset(power[:], -0.5))
                for n, norm in enumerate(norms):
                    for g in range(NORM_GROUPS):
                        pool.wait_ge(var_ready, n * NORM_GROUPS + g + 1)
                        link(nc.gpsimd.tensor_tensor(rstd[:, norm, tiles(g)], var[:, norm, tiles(g)],
                                                     power[:, tiles(g)], ALU.pow))
                        nc.gpsimd.tensor_tensor(shift[:, norm, tiles(g)], negmean[:, norm, tiles(g)],
                                                rstd[:, norm, tiles(g)], ALU.mult).then_inc(rstd_ready, 1)

            @block.vector
            def _(dve):
                link = linker(dve, chain)
                if x_loaded is not None:
                    dve.wait_ge(*x_loaded)

                def statistics(src, norm, g):
                    for t in range(g * NORM_TILES, (g + 1) * NORM_TILES):
                        last = nc.vector.bn_stats(stats[:, t, :], src[:, t, :])
                    link(last)
                    even_mean, even_m2 = stats[:, tiles(g), 1], stats[:, tiles(g), 2]
                    odd_mean, odd_m2 = stats[:, tiles(g), 4], stats[:, tiles(g), 5]
                    both, diff, m2, sq, total = (small[:, i, tiles(g)] for i in range(5))
                    nc.vector.tensor_tensor(both, even_mean, odd_mean, ALU.add)
                    nc.vector.tensor_tensor(m2, even_m2, odd_m2, ALU.add)
                    link(nc.vector.tensor_tensor(diff, even_mean, odd_mean, ALU.subtract))
                    nc.vector.tensor_scalar(negmean[:, norm, tiles(g)], both, -0.5, None, ALU.mult)
                    link(nc.vector.tensor_tensor(sq, diff, diff, ALU.mult))
                    link(nc.vector.scalar_tensor_tensor(total, sq, D / 4.0, m2, ALU.mult, ALU.add))
                    nc.vector.tensor_scalar(var[:, norm, tiles(g)], total, 1.0 / D, EPS, ALU.mult,
                                            ALU.add).then_inc(var_ready, 1)

                def low_parts(g):
                    for b in range(g * NORM_SEQS, (g + 1) * NORM_SEQS):
                        dve.wait_ge(hi_ready, b + 1)
                        nc.vector.tensor_tensor(xl[:, :, b * S:(b + 1) * S], turned[b % 2][:],
                                                xh[:, :, b * S:(b + 1) * S].bitcast(F32),
                                                ALU.subtract).then_inc(lo_ready, 1)

                if add_y:
                    for g in range(NORM_GROUPS):
                        statistics(y, 0, g)
                for g in range(NORM_GROUPS):
                    if add_y:
                        dve.wait_ge(y_scaled, g + 1)
                        ins = nc.vector.tensor_tensor(flat(x[:, tiles(g), :]), flat(x[:, tiles(g), :]),
                                                      flat(y[:, tiles(g), :]), ALU.add)
                        if make_norm:
                            link(ins)
                        else:
                            ins.then_inc(x_final, 1)
                    if make_norm:
                        statistics(x, 1, g)
                        if g >= 1 and not half:
                            low_parts(g - 1)
                if make_norm and not half:
                    low_parts(NORM_GROUPS - 1)

            @block.scalar
            def _(act):
                def scaled(dst, src, norm, t):
                    return nc.scalar.activation(dst, src, ACT.Identity, bias=shift[:, norm, t:t + 1],
                                                scale=rstd[:, norm, t:t + 1])

                def high_part(b):
                    act.wait_ge(xn_turned, b + 1)
                    nc.scalar.activation(xh[:, :, b * S:(b + 1) * S], turned[b % 2][:],
                                         ACT.Copy).then_inc(hi_ready, 1)

                if add_y:
                    for g in range(NORM_GROUPS):
                        act.wait_ge(rstd_ready, g + 1)
                        for t in range(g * NORM_TILES, (g + 1) * NORM_TILES):
                            last = scaled(y[:, t, :], y[:, t, :], 0, t)
                        last.then_inc(y_scaled, 1)
                if make_norm:
                    for b in range(B):
                        if b % NORM_SEQS == 0:
                            act.wait_ge(rstd_ready, x_base + b // NORM_SEQS + 1)
                        dst = xn16 if half else xn
                        scaled(dst[:, b % 2, 0, :], x[:, 2 * b, :], 1, 2 * b)
                        last = scaled(dst[:, b % 2, 1, :], x[:, 2 * b + 1, :], 1, 2 * b + 1)
                        if half:
                            last.then_inc(xn_rounded, 1)
                            act.wait_ge(xn_rounded, b + 1)
                            last = nc.scalar.activation(xn[:, b % 2, :, :], xn16[:, b % 2, :, :], ACT.Copy)
                        last.then_inc(xn_ready, 1)
                        if b >= 1:
                            high_part(b - 1)
                    high_part(B - 1)

            if make_norm:
                @block.tensor
                def _(pe):
                    for b in range(B):
                        pe.wait_ge(xn_ready, b + 1)
                        if b >= 2:
                            pe.wait_ge(hi_ready if half else lo_ready, b - 1)
                        for t in range(2):
                            for k in range(KD):
                                last = nc.tensor.transpose(turned[b % 2][:, k, t * P:(t + 1) * P],
                                                           xn[:, b % 2, t, k * P:(k + 1) * P], ident[:])
                        last.then_inc(xn_turned, 1)

            if out is not None:
                @block.sync
                def _(sp):
                    for g in range(NORM_GROUPS):
                        sp.wait_ge(x_final, g + 1)
                        sp.dma_start(out[:, tiles(g), :], x[:, tiles(g), :]).then_inc(stored, 16)
                    sp.wait_ge(stored, NORM_GROUPS * 16)



PAIRS = ((0, 0), (0, 1), (0, 2), (1, 0), (1, 1), (2, 0))
PARTS = 3
STACK = len(PAIRS) * HD + PARTS
VCOL = HD + 1 + 2 * HD
V_PARTS = ((0, HD + 1), (HD + 1, 2 * HD + 1), (2 * HD + 1, VCOL))


def stage_qkv(chip, xh, xl, vparts, qk_dram, ins):
    nc = chip.nc
    with ExitStack() as ctx:
        sb, pb = chip.memory(ctx)
        wraw = sb("wraw", [P, KD, 3 * D])
        wh = sb("wh", [P, KD, 3 * D], F32R)
        wl = sb("wl", [P, KD, 3 * D], F32R)
        bqk = sb("bqk", [P, 2 * KD])
        bqk_s = sb("bqk_s", [P, 2 * KD])
        bv = sb("bv", [P, D])
        whole = sb("whole", [P, 2, CHUNK])
        rest = sb("rest", [P, CHUNK])
        parts = sb("parts", [P, 2, PARTS, CHUNK], BF16)
        vwhole = sb("vwhole", [P, 2, D])
        vrest = sb("vrest", [P, D])
        pq = [pb(f"pq{n}", [P, CHUNK]) for n in range(3)]
        pv = [pb(f"pv{n}", [P, D]) for n in range(2)]
        loaded, raw_loaded, split_done = chip.sem("loaded"), chip.sem("raw_loaded"), chip.sem("split_done")
        bias_ready = chip.sem("bias_ready")
        qk_done, qk_whole, qk_link, qk_parts = (chip.sem(n) for n in ("qk_done", "qk_whole", "qk_link", "qk_parts"))
        qk_stored = [chip.sem("qk_stored") for _ in range(2)]
        v_done, v_link = chip.sem("v_done"), chip.sem("v_link")
        ones_set = chip.sem("ones_set")
        NB = 2 * KD
        with nc.Block() as block:
            @block.sync
            def _(sp):
                sp.dma_start(wraw[:], ins["wqkv"]).then_inc(raw_loaded, 16)
                sp.dma_start(bqk[:], ins["bqk"]).then_inc(loaded, 16)
                sp.dma_start(bv[:], ins["bv"]).then_inc(loaded, 16)
                for c in range(NCH):
                    for blk in range(NB):
                        n = c * NB + blk
                        sp.wait_ge(qk_parts, n + 1)
                        sp.dma_start(qk_dram[blk // KD, blk % KD, :, :, c * CHUNK:(c + 1) * CHUNK],
                                     parts[:, n % 2, :, :]).then_inc(qk_stored[n % 2], 16)
                for s in range(2):
                    sp.wait_ge(qk_stored[s], NCH * NB // 2 * 16)

            @block.gpsimd
            def _(pool):
                nc.gpsimd.memset(vparts[:], 1.0).then_inc(ones_set, 1)

            @block.tensor
            def _(pe):
                pe.wait_ge(split_done, 2)
                for c in range(NCH):
                    for blk in range(NB):
                        n = c * NB + blk
                        if n >= 3:
                            pe.wait_ge(qk_whole, n - 2)
                        terms = [(w, a, k) for k in range(KD) for w, a in ((wh, xh), (wh, xl), (wl, xh))]
                        for m, (w, a, k) in enumerate(terms):
                            last = nc.tensor.matmul(pq[n % 3][:], w[:, k, blk * P:(blk + 1) * P],
                                                    a[:, k, c * CHUNK:(c + 1) * CHUNK],
                                                    start=(m == 0), stop=(m == len(terms) - 1))
                        last.then_inc(qk_done, 1)
                    for t in range(c * TPC, (c + 1) * TPC):
                        if t >= 2:
                            pe.wait_ge(v_link, 5 * (t - 1) - 4)
                        terms = [(a, w, k) for k in range(KD) for a, w in ((xh, wh), (xh, wl), (xl, wh))]
                        for m, (a, w, k) in enumerate(terms):
                            last = nc.tensor.matmul(pv[t % 2][:], a[:, k, t * P:(t + 1) * P], w[:, k, 2 * D:],
                                                    start=(m == 0), stop=(m == len(terms) - 1))
                        last.then_inc(v_done, 1)

            @block.scalar
            def _(act):
                act.wait_ge(bias_ready, 1)
                for n in range(NCH * NB):
                    act.wait_ge(qk_done, n + 1)
                    if n >= 2:
                        act.wait_ge(qk_parts, n - 1)
                    blk = n % NB
                    scale = 1.0 / HD if blk < KD else 1.0
                    nc.scalar.activation(whole[:, n % 2, :], pq[n % 3][:], ACT.Identity,
                                         bias=bqk_s[:, blk:blk + 1], scale=scale).then_inc(qk_whole, 1)

            @block.vector
            def _(dve):
                dve.wait_ge(loaded, 32)
                nc.vector.tensor_scalar(bqk_s[:, 0:KD], bqk[:, 0:KD], 1.0 / HD, None, ALU.mult)
                nc.vector.tensor_copy(bqk_s[:, KD:], bqk[:, KD:]).then_inc(bias_ready, 1)
                dve.wait_ge(raw_loaded, 16)
                nc.vector.tensor_copy(flat(wh[:]), flat(wraw[:])).then_inc(split_done, 1)
                dve.wait_ge(split_done, 1)
                nc.vector.tensor_tensor(flat(wl[:]), flat(wraw[:]), flat(wh[:]).bitcast(F32),
                                        ALU.subtract).then_inc(split_done, 1)
                link = linker(dve, qk_link)
                vlink = linker(dve, v_link)
                dve.wait_ge(ones_set, 1)
                for c in range(NCH):
                    for blk in range(NB):
                        n = c * NB + blk
                        dve.wait_ge(qk_whole, n + 1)
                        if n >= 2:
                            dve.wait_ge(qk_stored[n % 2], n // 2 * 16)
                        w, p = whole[:, n % 2, :], parts[:, n % 2, :, :]
                        link(nc.vector.tensor_copy(p[:, 0, :], w))
                        link(nc.vector.tensor_tensor(rest[:], w, p[:, 0, :], ALU.subtract))
                        link(nc.vector.tensor_copy(p[:, 1, :], rest[:]))
                        nc.vector.tensor_tensor(p[:, 2, :], rest[:], p[:, 1, :], ALU.subtract).then_inc(qk_parts, 1)
                    for t in range(c * TPC, (c + 1) * TPC):
                        dve.wait_ge(v_done, t + 1)
                        dst = [vparts[:, t, :, a:a + HD] for a, _ in V_PARTS]

                        def heads(ap):
                            return ap.rearrange("p (h c) -> p h c", c=HD)

                        vlink(nc.vector.tensor_tensor(vwhole[:, t % 2, :], pv[t % 2][:], bv[:], ALU.add))
                        vlink(nc.vector.tensor_copy(dst[0], heads(vwhole[:, t % 2, :])))
                        vlink(nc.vector.tensor_tensor(heads(vrest[:]), heads(vwhole[:, t % 2, :]), dst[0],
                                                      ALU.subtract))
                        vlink(nc.vector.tensor_copy(dst[1], heads(vrest[:])))
                        vlink(nc.vector.tensor_tensor(dst[2], heads(vrest[:]), dst[1], ALU.subtract))


SLOTS = 4
WORK = 4
LAG_T, LAG_LO, LAG_V = 2, 3, 4
S_NORM, S_TURN, S_PROJ = 3, 5, 6
U_TURN, U_PROJ, USES = 5, 7, NH + 2


def work_use(s):
    return s if s < U_TURN else s + 1 if s == U_TURN else s + 2


def stage_attention(chip, vparts, qk_dram, y, ident, ins):
    nc = chip.nc
    STEPS = 2 * NH
    TURNS = B // 2
    LOADS = 2 * KD * len(PAIRS) + 1
    with ExitStack() as ctx:
        sb, pb = chip.memory(ctx)
        wproj = sb("wproj", [P, KD, D])
        bproj = sb("bproj", [P, D])
        identb = sb("identb", [P, P], BF16)
        mask = sb("mask", [P, P], BF16)
        stack = sb("stack", [STACK, 2, 2, NH, S], BF16)
        vs = sb("vs", [P, 2, 2, NH, VCOL], BF16)
        negmax = sb("negmax", [P, SLOTS, 2])
        prob = sb("prob", [P, SLOTS, 3 * P])
        probT_hi = sb("probT_hi", [P, SLOTS, 3 * P], F16)
        probT_lo = sb("probT_lo", [P, SLOTS, 3 * P], F16)
        rsum = sb("rsum", [P, 2, NH])
        on = sb("on", [P, 2, D])
        oT = sb("oT", [P, KD, S])
        work = [pb(f"work{n}", [P, 512]) for n in range(WORK)]
        pturn = [pb(f"pturn{n}", [P, 512]) for n in range(2)]
        acc = [pb(f"acc{n}", [P, 512]) for n in range(2)]
        acc_h = [a[:, 0:NH * (HD + 1)].rearrange("p (h c) -> p h c", c=HD + 1) for a in acc]
        loaded = chip.sem("loaded")
        in_loaded = [chip.sem("in_loaded") for _ in range(2)]
        scored, maxed, exped, p_turned = (chip.sem(n) for n in ("scored", "maxed", "exped", "p_turned"))
        hi_done, lo_done, pv_done = chip.sem("hi_done"), chip.sem("lo_done"), chip.sem("pv_done")
        inverted, normed, o_turned = chip.sem("inverted"), chip.sem("normed"), chip.sem("o_turned")
        o_copied, projected, y_ready = chip.sem("o_copied"), chip.sem("projected"), chip.sem("y_ready")

        def turns(eng, step):
            for st in range(STEPS):
                step(0, st, True, False)
            with eng.Fori(1, TURNS) as turn:
                for st in range(STEPS):
                    step(turn, st, False, False)
            for st in range(S_PROJ + 1):
                step(TURNS, st, False, True)

        def exists(h, first, tail):
            return not (first and h < 0) and not (tail and h >= 0)

        with nc.Block() as block:
            @block.sync
            def _(sp):
                for s in range(2):
                    sp.dma_start(stack[len(PAIRS) * HD:, s, :, :, :], ins["alibi"]).then_inc(loaded, 16)
                for dst, src in ((bproj, "bproj"), (identb, "identb"), (mask, "causal_add"), (wproj, "wproj")):
                    sp.dma_start(dst[:], ins[src]).then_inc(loaded, 16)

                def body(turn):
                    for s in range(2):
                        after(sp, scored, turn * STEPS - (1 - s) * NH)
                        for side in range(2):
                            for r, pair in enumerate(PAIRS):
                                for k in range(KD):
                                    src = qk_dram[side, k, :, pair[side], bass.ds(turn * (2 * S) + s * S, S)]
                                    half = slice(k * NH // KD, (k + 1) * NH // KD)
                                    sp.dma_start(stack[r * HD:(r + 1) * HD, s, side, half, :],
                                                 src.rearrange("(j c) l -> c j l", c=HD)).then_inc(in_loaded[s], 16)
                        after(sp, pv_done, turn * STEPS - (1 - s) * NH)
                        sp.dma_start(vs[:, s, :, :, :], vparts[:, bass.ds(turn * 4 + 2 * s, 2), :, :]
                                     ).then_inc(in_loaded[s], 16)

                body(0)
                with sp.Fori(1, TURNS) as turn:
                    body(turn)

            @block.tensor
            def _(pe):
                pe.wait_ge(loaded, 6 * 16)

                def bank_free(turn, st, use, first, tail):
                    n = st // NH * USES + use - WORK
                    if (first and n < 0) or (tail and n >= 0):
                        return
                    q, old = n // USES, n % USES
                    if old not in (U_TURN, U_PROJ):
                        head = old if old < U_TURN else old - 1 if old < U_PROJ else old - 2
                        pe.wait_ge(exped, turn * STEPS + (q * NH + head + 1))
                    elif not (first and q == 0):
                        pe.wait_ge(o_copied if old == U_TURN else y_ready, turn * 2 + q)

                def bank(st, use):
                    return work[(st // NH * USES + use) % WORK]

                def step(turn, st, first, tail):
                    s, slot = st % NH, st // NH
                    if not tail:
                        if s == 0:
                            pe.wait_ge(in_loaded[slot], turn * (16 * LOADS) + 16 * LOADS)
                        bank_free(turn, st, work_use(s), first, tail)
                        dst = bank(st, work_use(s))
                        q, k = stack[:, slot, 0, s, :], stack[:, slot, 1, s, :]
                        nc.tensor.matmul(dst[:, 0:P], q[:, 0:P], k[:, 0:P], start=True, stop=False)
                        nc.tensor.matmul(dst[:, 0:P], identb[:], mask[:], start=False, stop=True)
                        nc.tensor.matmul(dst[:, P:3 * P], q[:, P:S], k, start=True, stop=False,
                                         skip_group_check=True)
                        nc.tensor.matmul(dst[:, 2 * P:3 * P], identb[:], mask[:], start=False, stop=True,
                                         skip_group_check=True).then_inc(scored, 1)
                    h = st - LAG_T
                    if exists(h, first, tail):
                        pe.wait_ge(exped, turn * STEPS + (h + 1))
                        if exists(h - 2, first, tail):
                            pe.wait_ge(lo_done, turn * STEPS + (h - 1))
                        for m in range(3):
                            cols = slice(m * P, (m + 1) * P)
                            last = nc.tensor.transpose(pturn[h % 2][:, cols], prob[:, h % SLOTS, cols], ident[:])
                        last.then_inc(p_turned, 1)
                    h = st - LAG_V
                    if exists(h, first, tail):
                        pe.wait_ge(lo_done, turn * STEPS + (h + 1))
                        if h % NH == 0 and exists(h - NH, first, tail):
                            pe.wait_ge(normed, turn * 2 + h // NH)
                        for t, blocks in enumerate(((0,), (1, 2))):
                            terms = [(p, m, v) for m in blocks for p, v in
                                     ((probT_hi, 0), (probT_hi, 1), (probT_hi, 2), (probT_lo, 0), (probT_lo, 1))]
                            for i, (p, m, v) in enumerate(terms):
                                a, z = V_PARTS[v]
                                last = nc.tensor.matmul(acc_h[t][:, h % NH, 0:z - a],
                                                        p[:, h % SLOTS, m * P:(m + 1) * P],
                                                        vs[:, h // NH % 2, 1 if m == 2 else 0, h % NH, a:z],
                                                        start=(i == 0), stop=(i == len(terms) - 1),
                                                        skip_group_check=True)
                        last.then_inc(pv_done, 1)
                    if first and st < NH:
                        return
                    if s == S_TURN:
                        pe.wait_ge(normed, turn * 2 + slot)
                        bank_free(turn, st, U_TURN, first, tail)
                        for t in range(2):
                            for k in range(KD):
                                last = nc.tensor.transpose(bank(st, U_TURN)[:, k * S + t * P:k * S + (t + 1) * P],
                                                           on[:, t, k * P:(k + 1) * P], ident[:])
                        last.then_inc(o_turned, 1)
                    if s == S_PROJ:
                        pe.wait_ge(o_copied, turn * 2 + slot)
                        bank_free(turn, st, U_PROJ, first, tail)
                        for t in range(2):
                            for k in range(KD):
                                last = nc.tensor.matmul(bank(st, U_PROJ)[:, t * D:(t + 1) * D],
                                                        oT[:, k, t * P:(t + 1) * P], wproj[:, k, :],
                                                        start=(k == 0), stop=(k == KD - 1))
                        last.then_inc(projected, 1)

                turns(pe, step)

            def bank(st, use):
                return work[(st // NH * USES + use) % WORK]

            @block.scalar
            def _(act):
                def step(turn, st, first, tail):
                    if not tail:
                        src, r = bank(st, work_use(st % NH)), st % SLOTS
                        act.wait_ge(maxed, turn * STEPS + (st + 1))
                        if exists(st - SLOTS, first, tail):
                            act.wait_ge(p_turned, turn * STEPS + (st - SLOTS + 1))
                        nc.scalar.activation(prob[:, r, 0:P], src[:, 0:P], ACT.Exp, bias=negmax[:, r, 0:1])
                        nc.scalar.activation(prob[:, r, P:3 * P], src[:, P:3 * P], ACT.Exp,
                                             bias=negmax[:, r, 1:2]).then_inc(exped, 1)
                    h = st - LAG_T
                    if exists(h, first, tail):
                        act.wait_ge(p_turned, turn * STEPS + (h + 1))
                        if exists(h - SLOTS, first, tail):
                            act.wait_ge(pv_done, turn * STEPS + (h - SLOTS + 1))
                        nc.scalar.activation(probT_hi[:, h % SLOTS, :], pturn[h % 2][:, 0:3 * P],
                                             ACT.Copy).then_inc(hi_done, 1)
                    if st % NH == S_TURN and not (first and st < NH):
                        act.wait_ge(o_turned, turn * 2 + st // NH)
                        after(act, projected, turn * 2 + (st // NH - 1))
                        nc.scalar.activation(flat(oT[:]), bank(st, U_TURN)[:], ACT.Copy).then_inc(o_copied, 1)

                turns(act, step)

            @block.vector
            def _(dve):
                def step(turn, st, first, tail):
                    if not tail:
                        src, r = bank(st, work_use(st % NH)), st % SLOTS
                        dve.wait_ge(scored, turn * STEPS + (st + 1))
                        if exists(st - SLOTS, first, tail):
                            dve.wait_ge(exped, turn * STEPS + (st - SLOTS + 1))
                        nc.vector.tensor_reduce(negmax[:, r, 0:1], src[:, 0:P], AX.X, ALU.max, negate=True)
                        nc.vector.tensor_reduce(negmax[:, r, 1:2], src[:, P:3 * P], AX.X, ALU.max,
                                                negate=True).then_inc(maxed, 1)
                    h = st - LAG_LO
                    if exists(h, first, tail):
                        dve.wait_ge(hi_done, turn * STEPS + (h + 1))
                        nc.vector.tensor_tensor(probT_lo[:, h % SLOTS, :], pturn[h % 2][:, 0:3 * P],
                                                probT_hi[:, h % SLOTS, :], ALU.subtract).then_inc(lo_done, 1)
                    if first and st < NH:
                        return
                    seq = turn * 2 + st // NH
                    if st % NH == S_NORM:
                        dve.wait_ge(pv_done, turn * STEPS + st // NH * NH)
                        after(dve, o_turned, turn * 2 + (st // NH - 1))
                        for t in range(2):
                            last = nc.vector.reciprocal(rsum[:, t, :], acc_h[t][:, :, HD])
                        last.then_inc(inverted, 1)
                        dve.wait_ge(inverted, seq)
                        for t in range(2):
                            last = nc.vector.tensor_tensor(
                                on[:, t, :].rearrange("p (h c) -> p h c", c=HD), acc_h[t][:, :, 0:HD],
                                rsum[:, t, :].unsqueeze(2).broadcast_to([P, NH, HD]), ALU.mult)
                        last.then_inc(normed, 1)
                    if st % NH == S_PROJ:
                        dve.wait_ge(projected, seq)
                        nc.vector.tensor_tensor(y[:, bass.ds(seq * 2 - 2, 2), :],
                                                bank(st, U_PROJ)[:].rearrange("p (t n) -> p t n", n=D),
                                                bproj[:].unsqueeze(1).broadcast_to([P, 2, D]),
                                                ALU.add).then_inc(y_ready, 1)

                turns(dve, step)



GROUPS = 2
GCH = NCH // GROUPS
GT = NT // GROUPS


def stage_moe(chip, xh, xl, y, ident, ins):
    nc = chip.nc
    with ExitStack() as outer:
        sb, _ = chip.memory(outer)
        combT = sb("combT", [P, TOK], F32R)
        stage_router(chip, xh, xl, combT, ident, ins)
        stage_experts(chip, xh, xl, combT, y, ins)


def stage_router(chip, xh, xl, combT, ident, ins):
    nc = chip.nc
    TB = 8
    with ExitStack() as ctx:
        sb, pb = chip.memory(ctx)
        wraw = sb("wraw", [P, KD, NE])
        wh = sb("wh", [P, KD, NE], F32R)
        wl = sb("wl", [P, KD, NE], F32R)
        bias = sb("bias", [P, NE])
        logit = sb("logit", [P, NT, NE])
        ranked = sb("ranked", [P, NT, NE + TOPK])
        best = sb("best", [P, NT, 8])
        left = sb("left", [P, NT, NE + TOPK])
        chosen = sb("chosen", [P, NT, NE])
        expd = sb("expd", [P, NT, NE])
        top = sb("top", [P, NT])
        total = sb("total", [P, NT])
        inv = sb("inv", [P, NT])
        ps = [pb(f"logits{n}", [P, TB, NE]) for n in range(2)]
        pt = [pb(f"combined{n}", [P, CHUNK]) for n in range(2)]
        loaded, chain = chip.sem("loaded"), chip.sem("router_chain")
        split_done, logits_done = chip.sem("split_done"), chip.sem("logits_done")
        shifted, exp_done = chip.sem("shifted"), chip.sem("exp_done")
        comb_done, turned = chip.sem("comb_done"), chip.sem("turned")
        hi_done, lo_done = chip.sem("hi_done"), chip.sem("lo_done")
        with nc.Block() as block:
            @block.sync
            def _(sp):
                sp.dma_start(wraw[:], ins["router_w"]).then_inc(loaded, 16)
                sp.dma_start(bias[:], ins["router_b"]).then_inc(loaded, 16)

            @block.tensor
            def _(pe):
                pe.wait_ge(split_done, 2)
                parts = [(a, w, k) for k in range(KD) for a, w in ((xh, wh), (xh, wl), (xl, wh))]
                for t in range(NT):
                    for m, (a, w, k) in enumerate(parts):
                        last = nc.tensor.matmul(ps[t // TB][:, t % TB, :], a[:, k, t * P:(t + 1) * P], w[:, k, :],
                                                start=(m == 0), stop=(m == len(parts) - 1))
                    if t % TB == TB - 1:
                        last.then_inc(logits_done, 1)
                pe.wait_ge(comb_done, 1)
                for c in range(NCH):
                    if c >= 2:
                        pe.wait_ge(lo_done, c - 1)
                    for n in range(TPC):
                        last = nc.tensor.transpose(pt[c % 2][0:NE, n * P:(n + 1) * P], expd[:, c * TPC + n, :],
                                                   ident[:])
                    last.then_inc(turned, 1)

            @block.scalar
            def _(act):
                act.wait_ge(shifted, 1)
                nc.scalar.activation(flat(expd[:]), flat(logit[:]), ACT.Exp).then_inc(exp_done, 1)

            @block.vector
            def _(dve):
                link = linker(dve, chain)
                dve.wait_ge(loaded, 32)
                nc.vector.tensor_copy(flat(wh[:]), flat(wraw[:])).then_inc(split_done, 1)
                dve.wait_ge(split_done, 1)
                nc.vector.tensor_tensor(flat(wl[:]), flat(wraw[:]), flat(wh[:]).bitcast(F32),
                                        ALU.subtract).then_inc(split_done, 1)
                nc.vector.memset(ranked[:, :, NE:], BIG)
                for n in range(NT // TB):
                    tiles = slice(n * TB, (n + 1) * TB)
                    dve.wait_ge(logits_done, n + 1)
                    nc.vector.tensor_copy(logit[:, tiles, :], ps[n][:])
                    link(nc.vector.tensor_tensor(ranked[:, tiles, 0:NE], ps[n][:],
                                                 bias[:].unsqueeze(1).broadcast_to([P, TB, NE]), ALU.add))
                link(nc.vector.tensor_reduce(top[:], logit[:], AX.X, ALU.max))
                link(nc.vector.tensor_tensor(logit[:], logit[:], top[:].unsqueeze(2).broadcast_to([P, NT, NE]),
                                             ALU.subtract))
                nc.vector.sem_inc(shifted, 1)
                for t in range(NT):
                    last = nc.vector.max(best[:, t, :], ranked[:, t, :])
                link(last)
                for t in range(NT):
                    last = nc.vector.match_replace(left[:, t, :], best[:, t, :], ranked[:, t, :], -BIG)
                link(last)
                link(nc.vector.tensor_tensor(chosen[:], ranked[:, :, 0:NE], left[:, :, 0:NE], ALU.not_equal))
                dve.wait_ge(exp_done, 1)
                link(nc.vector.tensor_tensor(flat(expd[:]), flat(expd[:]), flat(chosen[:]), ALU.mult))
                link(nc.vector.tensor_reduce(total[:], expd[:], AX.X, ALU.add))
                link(nc.vector.reciprocal(inv[:], total[:]))
                nc.vector.tensor_tensor(expd[:], expd[:], inv[:].unsqueeze(2).broadcast_to([P, NT, NE]),
                                        ALU.mult).then_inc(comb_done, 1)
                for c in range(NCH):
                    cols = slice(c * CHUNK, (c + 1) * CHUNK)
                    dve.wait_ge(turned, c + 1)
                    nc.vector.tensor_copy(combT[0:NE, cols], pt[c % 2][0:NE, :]).then_inc(hi_done, 1)
                    dve.wait_ge(hi_done, c + 1)
                    nc.vector.tensor_tensor(combT[NE:2 * NE, cols], pt[c % 2][0:NE, :],
                                            combT[0:NE, cols].bitcast(F32), ALU.subtract).then_inc(lo_done, 1)


def stage_experts(chip, xh, xl, combT, y, ins):
    nc = chip.nc
    WCOL = WBLK + P
    TURNS_R, TURNS_S = ROUTED // 2, SHARED // 2
    TURNS = TURNS_R + TURNS_S
    STEPS = 2 * GCH
    with ExitStack() as ctx:
        sb, pb = chip.memory(ctx)
        wraw = sb("wraw", [P, 2, WCOL])
        wh = sb("wh", [P, 2, WCOL], F32R)
        wl = sb("wl", [P, 2, WBLK], F32R)
        gate = sb("gate", [P, 2, CHUNK])
        prod = sb("prod", [P, 2, CHUNK])
        hid = sb("hid", [P, 2, CHUNK])
        hh = sb("hh", [P, 2, CHUNK], F32R)
        hl = sb("hl", [P, 2, CHUNK], F32R)
        zeros = sb("zeros", [P, CHUNK], BF16)
        none = sb("none", [P, 1])
        pg, pu, pc = pb("pg", [P, CHUNK]), pb("pu", [P, CHUNK]), pb("pc", [P, CHUNK])
        acc = [pb(f"acc{n}", [P, 2, D]) for n in range(GT // 2)]
        zeroed, none_set = chip.sem("zeroed"), chip.sem("none_set")
        w_loaded = [chip.sem("w_loaded") for _ in range(2)]
        w_half, w_split = chip.sem("w_half"), chip.sem("w_split")
        gate_done, up_done, comb_done = chip.sem("gate_done"), chip.sem("up_done"), chip.sem("comb_done")
        silu_done, prod_done, hid_done = chip.sem("silu_done"), chip.sem("prod_done"), chip.sem("hid_done")
        hi_done, lo_done = chip.sem("hi_done"), chip.sem("lo_done")
        down_done, y_out = chip.sem("down_done"), chip.sem("y_out")

        def turns(eng, body):
            for g in range(GROUPS):
                body(g * TURNS, g, True, True)
                with eng.Fori(g * TURNS + 1, g * TURNS + TURNS_R) as i:
                    body(i, g, True, False)
                with eng.Fori(g * TURNS + TURNS_R, (g + 1) * TURNS) as i:
                    body(i, g, False, False)
                yield g

        with nc.Block() as block:
            @block.sync
            def _(sp):
                def load(i, g):
                    for s in range(2):
                        if g or not isinstance(i, int):
                            sp.wait_ge(w_split, (i + g * TURNS) * 2 + (s - 1))
                        sp.dma_start(wraw[:, s, :], ins["experts"][bass.ds(i * 2 + s, 1), :, :]
                                     .rearrange("a p n -> p (a n)")).then_inc(w_loaded[s], 16)

                for g in range(GROUPS):
                    load(0, g)
                    with sp.Fori(1, TURNS) as i:
                        load(i, g)

            @block.gpsimd
            def _(pool):
                nc.gpsimd.memset(zeros[:], 0.0).then_inc(zeroed, 1)
                nc.gpsimd.memset(none[:], 0.0).then_inc(none_set, 1)
                pool.wait_ge(none_set, 1)

                def split(i):
                    for s in range(2):
                        pool.wait_ge(w_loaded[s], i * 16 + 16)
                        if not isinstance(i, int):
                            pool.wait_ge(down_done, i * (2 * GCH) + (s - 1) * GCH)
                        nc.gpsimd.tensor_tensor(wh[:, s, :], wraw[:, s, :],
                                                none[:].broadcast_to([P, WCOL]), ALU.add).then_inc(w_half, 1)
                        pool.wait_ge(w_half, i * 2 + (s + 1))
                        nc.gpsimd.tensor_tensor(wl[:, s, :], wraw[:, s, 0:WBLK], wh[:, s, 0:WBLK].bitcast(F32),
                                                ALU.subtract).then_inc(w_split, 1)

                split(0)
                with pool.Fori(1, GROUPS * TURNS) as i:
                    split(i)

            @block.tensor
            def _(pe):
                pe.wait_ge(zeroed, 1)

                def hidden(bank, s, col, g, c, done):
                    tok = slice((g * GCH + c) * CHUNK, (g * GCH + c + 1) * CHUNK)
                    parts = [(w, a, k) for k in range(KD) for w, a in ((wh, xh), (wh, xl), (wl, xh))]
                    for m, (w, a, k) in enumerate(parts):
                        last = nc.tensor.matmul(bank[:], w[:, s, col + k * P:col + (k + 1) * P], a[:, k, tok],
                                                start=(m == 0), stop=(m == len(parts) - 1))
                    last.then_inc(done, 1)

                def down(st, count):
                    s, c = st // GCH, st % GCH
                    pe.wait_ge(lo_done, count)
                    for t in range(TPC):
                        tile = c * TPC + t
                        for a, w in ((hh, wh), (hh, wl), (hl, wh)):
                            last = nc.tensor.matmul(acc[tile // 2][:, tile % 2, :], a[:, st % 2, t * P:(t + 1) * P],
                                                    w[:, s, 2 * D:3 * D], start=False, stop=False,
                                                    skip_group_check=True)
                    last.then_inc(down_done, 1)

                def body(turn, g, routed, first):
                    for st in range(STEPS):
                        s, c = st // GCH, st % GCH
                        if c == 0:
                            pe.wait_ge(w_split, turn * 2 + (s + 1))
                        after(pe, silu_done, turn * STEPS + st)
                        hidden(pg, s, 0, g, c, gate_done)
                        after(pe, prod_done, turn * STEPS + st)
                        hidden(pu, s, D, g, c, up_done)
                        if routed:
                            after(pe, hid_done, turn * STEPS + st)
                            tok = slice((g * GCH + c) * CHUNK, (g * GCH + c + 1) * CHUNK)
                            nc.tensor.matmul(pc[:], wh[:, s, WBLK:WCOL], combT[:, tok], start=True,
                                             stop=True).then_inc(comb_done, 1)
                        if not (first and st == 0):
                            down((st - 1) % STEPS, turn * STEPS + st)

                def group(g):
                    if g:
                        pe.wait_ge(y_out, g * len(acc))
                    for a in acc:
                        nc.tensor.matmul(flat(a[:]), zeros[:, 0:P], zeros[:], start=True, stop=False,
                                         skip_group_check=True)

                group(0)
                for g in turns(pe, body):
                    down(STEPS - 1, (g + 1) * TURNS * STEPS)
                    if g + 1 < GROUPS:
                        group(g + 1)

            @block.scalar
            def _(act):
                def body(turn, g, routed, first):
                    for st in range(STEPS):
                        n = turn * STEPS + (st + 1)
                        act.wait_ge(gate_done, n)
                        nc.scalar.activation(gate[:, st % 2, :], pg[:], ACT.Silu).then_inc(silu_done, 1)
                        act.wait_ge(hid_done, n)
                        nc.scalar.activation(hh[:, st % 2, :], hid[:, st % 2, :], ACT.Copy).then_inc(hi_done, 1)

                for g in turns(act, body):
                    act.wait_ge(down_done, (g + 1) * TURNS * STEPS)
                    for n in range(0, len(acc), 2):
                        nc.scalar.activation(y[:, g * GT + 2 * n:g * GT + 2 * n + 2, :], acc[n][:],
                                             ACT.Copy).then_inc(y_out, 1)

            @block.vector
            def _(dve):
                def body(turn, g, routed, first):
                    for st in range(STEPS):
                        n = turn * STEPS + (st + 1)
                        dve.wait_ge(silu_done, n)
                        dve.wait_ge(up_done, n)
                        nc.vector.tensor_tensor(prod[:, st % 2, :], gate[:, st % 2, :], pu[:],
                                                ALU.mult).then_inc(prod_done, 1)
                        dve.wait_ge(prod_done, n)
                        if routed:
                            dve.wait_ge(comb_done, n - g * TURNS_S * STEPS)
                            ins_ = nc.vector.tensor_tensor(hid[:, st % 2, :], prod[:, st % 2, :], pc[:], ALU.mult)
                        else:
                            ins_ = nc.vector.tensor_copy(hid[:, st % 2, :], prod[:, st % 2, :])
                        ins_.then_inc(hid_done, 1)
                        dve.wait_ge(hi_done, n)
                        nc.vector.tensor_tensor(hl[:, st % 2, :], hid[:, st % 2, :],
                                                hh[:, st % 2, :].bitcast(F32), ALU.subtract).then_inc(lo_done, 1)

                for g in turns(dve, body):
                    dve.wait_ge(down_done, (g + 1) * TURNS * STEPS)
                    for n in range(1, len(acc), 2):
                        nc.vector.tensor_copy(y[:, g * GT + 2 * n:g * GT + 2 * n + 2, :],
                                              acc[n][:]).then_inc(y_out, 1)



TAPS = 4
CB_IN = 2 * NC + 1


def stage_ssm(chip, xh, xl, y, ident, ins):
    with ExitStack() as outer:
        sb, _ = chip.memory(outer)
        t = {
            "val": sb("val", [P, NT, DI]),
            "gateT": sb("gateT", [P, NC, TOK]),
        }
        with ExitStack() as mid:
            sb, _ = chip.memory(mid)
            t["ecum"] = sb("ecum", [P, NT, SH])
            t["erem"] = sb("erem", [P, NT, SH])
            t["negcum"] = sb("negcum", [P, NT, SH])
            t["cparts"] = sb("cparts", [PARTS * SH, TOK], BF16)
            stage_ssm_in(chip, xh, xl, t, ident, ins)
            stage_ssm_heads(chip, xh, xl, t, ins)
        stage_ssm_out(chip, t, y, ident, ins)


def stage_ssm_in(chip, xh, xl, t, ident, ins):
    nc = chip.nc
    val, gateT = t["val"], t["gateT"]
    with ExitStack() as ctx:
        sb, pb = chip.memory(ctx)
        z = sb("z", [SH, TOK])
        ld_tok = sb("ld_tok", [P, NT, SH])
        tri = sb("tri", [P, 2, P])
        chan = sb("chan", [P, NC, TAPS + 1])
        head = sb("head", [SH, 2])
        rate = sb("rate", [SH, 1])
        loaded = chip.sem("loaded")
        with ExitStack() as inner:
            sb, pb = chip.memory(inner)
            wraw = sb("wraw", [P, KD, CB_IN * P])
            wh = sb("wh", [P, KD, CB_IN * P], F32R)
            wl = sb("wl", [P, KD, CB_IN * P], F32R)
            pad = sb("pad", [P, 2, CHUNK // S, TAPS - 1 + S])
            conv = sb("conv", [P, 2, CHUNK // S, S])
            valT = sb("valT", [P, 2, CHUNK])
            pin = [pb(f"pin{n}", [P, CHUNK]) for n in range(3)]
            pv = [pb(f"pv{n}", [P, CHUNK]) for n in range(2)]
            raw_loaded, split_done = chip.sem("raw_loaded"), chip.sem("split_done")
            padded = chip.sem("padded")
            proj_done, taken = chip.sem("proj_done"), chip.sem("taken")
            conv_link, conv_done = chip.sem("conv_link"), chip.sem("conv_done")
            silu_done, val_turned, val_out = chip.sem("silu_done"), chip.sem("val_turned"), chip.sem("val_out")
            with nc.Block() as block:
                @block.sync
                def _(sp):
                    sp.dma_start(wraw[:], ins["w_in"]).then_inc(raw_loaded, 16)
                    for dst, src in ((tri, "tri"), (chan, "chan"), (head, "head")):
                        sp.dma_start(dst[:], ins[src]).then_inc(loaded, 16)

                @block.gpsimd
                def _(pool):
                    nc.gpsimd.memset(pad[:], 0.0).then_inc(padded, 1)

                @block.tensor
                def _(pe):
                    pe.wait_ge(split_done, 2)
                    parts = [(w, a, k) for k in range(KD) for w, a in ((wh, xh), (wh, xl), (wl, xh))]
                    def body(c):
                        for blk in range(CB_IN + 1):
                            if blk < CB_IN:
                                if blk < 3:
                                    after(pe, taken, c * CB_IN)
                                else:
                                    pe.wait_ge(taken, c * CB_IN + (blk - 2))
                                for m, (w, a, k) in enumerate(parts):
                                    last = nc.tensor.matmul(pin[blk % 3][:], w[:, k, blk * P:(blk + 1) * P],
                                                            a[:, k, bass.ts(c, CHUNK)],
                                                            start=(m == 0), stop=(m == len(parts) - 1))
                                last.then_inc(proj_done, 1)
                            if 2 <= blk < 2 + NC:
                                v = blk - 2
                                pe.wait_ge(silu_done, c * NC + (v + 1))
                                if v >= 2:
                                    pe.wait_ge(val_out, c * NC + (v - 1))
                                else:
                                    after(pe, val_out, c * NC)
                                for n in range(TPC):
                                    last = nc.tensor.transpose(pv[v % 2][:, n * P:(n + 1) * P],
                                                               valT[:, v % 2, n * P:(n + 1) * P], ident[:])
                                last.then_inc(val_turned, 1)

                    repeat(pe, NCH, body)

                @block.scalar
                def _(act):
                    act.wait_ge(loaded, 3 * 16)
                    act.wait_ge(padded, 1)
                    def body(c):
                        for blk in range(CB_IN):
                            act.wait_ge(proj_done, c * CB_IN + (blk + 1))
                            src = pin[blk % 3]
                            if blk < NC:
                                if blk >= 2:
                                    act.wait_ge(conv_done, c * NC + (blk - 1))
                                ins_ = nc.scalar.activation(pad[:, blk % 2, :, TAPS - 1:],
                                                            src[:].rearrange("p (b s) -> p b s", s=S), ACT.Copy)
                            elif blk < 2 * NC:
                                ins_ = nc.scalar.activation(gateT[:, blk - NC, bass.ts(c, CHUNK)], src[:], ACT.Silu)
                            else:
                                ins_ = nc.scalar.activation(z[:, bass.ts(c, CHUNK)], src[0:SH, :], ACT.Identity,
                                                            bias=head[:, 0:1])
                            ins_.then_inc(taken, 1)
                            if 1 <= blk < 1 + NC:
                                v = blk - 1
                                act.wait_ge(conv_done, c * NC + (v + 1))
                                if v >= 2:
                                    act.wait_ge(val_turned, c * NC + (v - 1))
                                nc.scalar.activation(valT[:, v % 2, :], conv[:, v % 2, :, :]
                                                     .rearrange("p b s -> p (b s)"), ACT.Silu).then_inc(silu_done, 1)

                    repeat(act, NCH, body)

                @block.vector
                def _(dve):
                    dve.wait_ge(raw_loaded, 16)
                    nc.vector.tensor_copy(flat(wh[:]), flat(wraw[:])).then_inc(split_done, 1)
                    dve.wait_ge(split_done, 1)
                    nc.vector.tensor_tensor(flat(wl[:]), flat(wraw[:]), flat(wh[:]).bitcast(F32),
                                            ALU.subtract).then_inc(split_done, 1)
                    dve.wait_ge(loaded, 3 * 16)
                    def body(c):
                        for blk in range(NC + 1):
                            if blk < NC:
                                dve.wait_ge(taken, c * CB_IN + (blk + 1))
                                if blk >= 2:
                                    dve.wait_ge(silu_done, c * NC + (blk - 1))
                                dst = conv[:, blk % 2, :, :]
                                nc.vector.tensor_scalar(dst, pad[:, blk % 2, :, TAPS - 1:TAPS - 1 + S],
                                                        chan[:, blk, TAPS - 1:TAPS], chan[:, blk, TAPS:TAPS + 1],
                                                        ALU.mult, ALU.add).then_inc(conv_link, 1)
                                for k in range(TAPS - 2, -1, -1):
                                    dve.wait_ge(conv_link, c * (NC * (TAPS - 1)) + (blk * (TAPS - 1) + TAPS - 1 - k))
                                    last = nc.vector.scalar_tensor_tensor(dst, pad[:, blk % 2, :, k:k + S],
                                                                          chan[:, blk, k:k + 1], dst,
                                                                          ALU.mult, ALU.add)
                                    last.then_inc(conv_link if k else conv_done, 1)
                            if blk >= 1:
                                v = blk - 1
                                dve.wait_ge(val_turned, c * NC + (v + 1))
                                nc.vector.tensor_copy(val[:, bass.ts(c, TPC), v * P:(v + 1) * P],
                                                      pv[v % 2][:].rearrange("p (t n) -> p t n", n=P)
                                                      ).then_inc(val_out, 1)

                    repeat(dve, NCH, body)

        with ExitStack() as inner:
            sb, pb = chip.memory(inner)
            soft = sb("soft", [SH, TOK])
            cum = sb("cum", [SH, CHUNK])
            part = sb("part", [SH, CHUNK], BF16)
            pt = pb("pt", [P, NT, SH])
            pcum, prem = pb("pcum", [P, NT * SH]), pb("prem", [P, NT * SH])
            pcT = [pb(f"pcT{n}", [SH, CHUNK]) for n in range(NCH)]
            act_link, chain = chip.sem("act_link"), chip.sem("decay_chain")
            soft_done, ld_done, ld_turned = chip.sem("soft_done"), chip.sem("ld_done"), chip.sem("ld_turned")
            ld_copied, sums_done, exps_done = chip.sem("ld_copied"), chip.sem("sums_done"), chip.sem("exps_done")
            with nc.Block() as block:
                @block.scalar
                def _(act):
                    link = linker(act, act_link)
                    link(nc.scalar.activation(rate[:], head[:, 1:2], ACT.Exp))
                    link(nc.scalar.activation(soft[:], z[:], ACT.Abs))
                    link(nc.scalar.activation(soft[:], soft[:], ACT.Exp, scale=-1.0))
                    link(nc.scalar.activation(soft[:], soft[:], ACT.Ln, bias=1.0))
                    nc.scalar.sem_inc(soft_done, 1)
                    act.wait_ge(sums_done, 1)
                    nc.scalar.activation(flat(t["ecum"][:]), pcum[:], ACT.Exp)
                    nc.scalar.activation(flat(t["erem"][:]), prem[:], ACT.Exp).then_inc(exps_done, 1)

                @block.vector
                def _(dve):
                    link = linker(dve, chain)
                    dve.wait_ge(soft_done, 1)
                    link(nc.vector.scalar_tensor_tensor(z[:], z[:], 0.0, soft[:], ALU.max, ALU.add))
                    nc.vector.tensor_scalar(z[:], z[:], rate[:, 0:1], -1.0, ALU.mult, ALU.mult).then_inc(ld_done, 1)
                    dve.wait_ge(ld_turned, 1)
                    nc.vector.tensor_copy(ld_tok[:], pt[:]).then_inc(ld_copied, 1)
                    dve.wait_ge(exps_done, 1)
                    nc.vector.tensor_scalar(flat(t["negcum"][:]), pcum[:], -1.0, None, ALU.mult)
                    dve.wait_ge(sums_done, 2)
                    for c in range(NCH):
                        cols = slice(c * CHUNK, (c + 1) * CHUNK)
                        link(nc.vector.tensor_copy(t["cparts"][0:SH, cols], pcT[c][:]))
                        link(nc.vector.tensor_tensor(cum[:], pcT[c][:], t["cparts"][0:SH, cols], ALU.subtract))
                        link(nc.vector.tensor_copy(part[:], cum[:]))
                        nc.vector.tensor_copy(t["cparts"][SH:2 * SH, cols], part[:])
                        link(nc.vector.tensor_tensor(cum[:], cum[:], part[:], ALU.subtract))
                        link(nc.vector.tensor_copy(t["cparts"][2 * SH:3 * SH, cols], cum[:]))

                @block.tensor
                def _(pe):
                    pe.wait_ge(ld_done, 1)
                    for n in range(NT):
                        last = nc.tensor.transpose(pt[:, n, :], z[:, n * P:(n + 1) * P], ident[0:SH, 0:SH])
                    last.then_inc(ld_turned, 1)
                    pe.wait_ge(ld_copied, 1)
                    nc.tensor.matmul(pcum[:], tri[:, 0, :], flat(ld_tok[:]), start=True, stop=True)
                    nc.tensor.matmul(prem[:], tri[:, 1, :], flat(ld_tok[:]), start=True,
                                     stop=True).then_inc(sums_done, 1)
                    for n in range(NT):
                        last = nc.tensor.matmul(pcT[n // TPC][:, (n % TPC) * P:(n % TPC + 1) * P], ld_tok[:, n, :],
                                                tri[:, 0, :], start=True, stop=True)
                    last.then_inc(sums_done, 1)


def stage_ssm_heads(chip, xh, xl, t, ins):
    nc = chip.nc
    val, ecum, erem, cparts, negcum = t["val"], t["ecum"], t["erem"], t["cparts"], t["negcum"]
    WCOL = 2 * KD * P
    BPC = CHUNK // S
    STEPS = 2 * NCH
    TURNS = SH // 2
    ROWS = PARTS * SH
    with ExitStack() as ctx:
        sb, pb = chip.memory(ctx)
        wraw = sb("wraw", [P, 2, WCOL])
        wh = sb("wh", [P, 2, WCOL], F32R)
        wl = sb("wl", [P, 2, WCOL], F32R)
        sel = sb("sel", [ROWS, SH * P], BF16)
        mask = sb("mask", [P, TPC * P])
        skip = sb("skip", [P, DI])
        bT = sb("bT", [P, 2, CHUNK])
        cT = sb("cT", [P, 2, CHUNK])
        masked = sb("masked", [P, 2, CHUNK])
        decay = sb("decay", [P, 2, CHUNK])
        mixT = sb("mixT", [P, 2, TPC, P])
        cross = sb("cross", [P, 2, BPC, P])
        vdec = sb("vdec", [P, 2, B, SHD])
        vskip = sb("vskip", [P, 2, NT, SHD])
        late = sb("late", [P, B, SHD])
        none = sb("none", [P, 1])
        pbT, pcT, pdec = pb("pbT", [P, CHUNK]), pb("pcT", [P, CHUNK]), pb("pdec", [P, CHUNK])
        pcb = [pb(f"pcb{n}", [P, 3, P]) for n in range(BPC)]
        py = [pb(f"py{n}", [P, NT + B, SHD]) for n in range(2)]
        loaded = chip.sem("loaded")
        w_loaded = [chip.sem("w_loaded") for _ in range(2)]
        w_half, w_split = chip.sem("w_half"), chip.sem("w_split")
        b_done, c_done, dec_done = chip.sem("b_done"), chip.sem("c_done"), chip.sem("dec_done")
        b_out, c_out, dec_out = chip.sem("b_out"), chip.sem("c_out"), chip.sem("dec_out")
        dec_masked = chip.sem("dec_masked")
        cb_done, mix_out, cross_out = chip.sem("cb_done"), chip.sem("mix_out"), chip.sem("cross_out")
        y_done, late_out, y_out = chip.sem("y_done"), chip.sem("late_out"), chip.sem("y_out")
        v_ready, none_set = chip.sem("v_ready"), chip.sem("none_set")

        def turns(eng, body):
            body(0, True)
            with eng.Fori(1, TURNS) as i:
                body(i, False)

        def head_cols(turn, hp):
            return bass.ds(turn * (2 * SHD) + hp * SHD, SHD)

        with nc.Block() as block:
            @block.sync
            def _(sp):
                for dst, src in ((sel, "head_rows"), (mask, "mask_turned"), (skip, "skip")):
                    sp.dma_start(dst[:], ins[src]).then_inc(loaded, 16)

                def body(turn, first):
                    for s in range(2):
                        if not first:
                            sp.wait_ge(w_split, turn * 2 + (s - 1))
                        sp.dma_start(wraw[:, s, :], ins["w_bc"][bass.ds(turn * 2 + s, 1), :, :]
                                     .rearrange("a p n -> p (a n)")).then_inc(w_loaded[s], 16)

                turns(sp, body)

            @block.gpsimd
            def _(pool):
                nc.gpsimd.memset(none[:], 0.0).then_inc(none_set, 1)
                pool.wait_ge(none_set, 1)
                pool.wait_ge(loaded, 3 * 16)

                def body(turn, first):
                    for s in range(2):
                        pool.wait_ge(w_loaded[s], turn * 16 + 16)
                        if not first:
                            pool.wait_ge(c_done, turn * STEPS + (s - 1) * NCH)
                        nc.gpsimd.tensor_tensor(wh[:, s, :], wraw[:, s, :],
                                                none[:].broadcast_to([P, WCOL]), ALU.add).then_inc(w_half, 1)
                        pool.wait_ge(w_half, turn * 2 + (s + 1))
                        nc.gpsimd.tensor_tensor(wl[:, s, :], wraw[:, s, :], wh[:, s, :].bitcast(F32),
                                                ALU.subtract).then_inc(w_split, 1)
                        if not first:
                            pool.wait_ge(y_out, turn * 2 + (s - 1))
                        cols = head_cols(turn, s)
                        head = bass.ds(turn * 2 + s, 1)
                        nc.gpsimd.tensor_tensor(vdec[:, s, :, :], val[:, 0:NT:2, cols],
                                                erem[:, 0:NT:2, head].broadcast_to([P, B, SHD]), ALU.mult)
                        nc.gpsimd.tensor_tensor(vskip[:, s, :, :], val[:, :, cols],
                                                skip[:, cols].unsqueeze(1).broadcast_to([P, NT, SHD]),
                                                ALU.mult).then_inc(v_ready, 1)

                turns(pool, body)

            @block.tensor
            def _(pe):
                pe.wait_ge(loaded, 3 * 16)

                def project(bank, s, what, c, done):
                    parts = [(w, a, k) for k in range(KD) for w, a in ((wh, xh), (wh, xl), (wl, xh))]
                    for m, (w, a, k) in enumerate(parts):
                        col = (what * KD + k) * P
                        last = nc.tensor.matmul(bank[:], w[:, s, col:col + P], a[:, k, c * CHUNK:(c + 1) * CHUNK],
                                                start=(m == 0), stop=(m == len(parts) - 1))
                    last.then_inc(done, 1)

                def decays(turn, s, c):
                    head = bass.ds(turn * (2 * P) + s * P, P)
                    nc.tensor.matmul(pdec[:], sel[:, head], cparts[:, c * CHUNK:(c + 1) * CHUNK],
                                     start=True, stop=True).then_inc(dec_done, 1)

                def products(st, count):
                    pe.wait_ge(b_out, count)
                    pe.wait_ge(c_out, count)
                    for q in range(BPC):
                        o = q * S
                        nc.tensor.matmul(pcb[q][:, 0:2, :], bT[:, st % 2, o:o + P], cT[:, st % 2, o:o + S],
                                         start=True, stop=True)
                        last = nc.tensor.matmul(pcb[q][:, 2, :], bT[:, st % 2, o + P:o + S],
                                                cT[:, st % 2, o + P:o + S], start=True, stop=True)
                    last.then_inc(cb_done, 1)

                def outputs(turn, st, count):
                    s, c = st // NCH, st % NCH
                    pe.wait_ge(mix_out, count)
                    pe.wait_ge(cross_out, count)
                    cols = head_cols(turn, s)
                    for n in range(TPC):
                        tile = c * TPC + n
                        nc.tensor.matmul(py[s][:, tile, :], mixT[:, st % 2, n, :], val[:, tile, cols],
                                         start=True, stop=True)
                    for q in range(BPC):
                        seq = c * BPC + q
                        last = nc.tensor.matmul(py[s][:, NT + seq, :], cross[:, st % 2, q, :], vdec[:, s, seq, :],
                                                start=True, stop=True)
                    last.then_inc(y_done, 1)

                def body(turn, first):
                    for st in range(STEPS):
                        s, c = st // NCH, st % NCH
                        if c == 0:
                            pe.wait_ge(w_split, turn * 2 + (s + 1))
                        after(pe, b_out, turn * STEPS + st)
                        project(pbT, s, 0, c, b_done)
                        after(pe, dec_masked, turn * STEPS + st)
                        decays(turn, s, c)
                        after(pe, c_out, turn * STEPS + st)
                        project(pcT, s, 1, c, c_done)
                        if not (first and st < 2):
                            pe.wait_ge(mix_out, turn * STEPS + (st - 1))
                            pe.wait_ge(cross_out, turn * STEPS + (st - 1))
                        if not (first and st == 0):
                            products((st - 1) % STEPS, turn * STEPS + st)
                        if not (first and st < 2):
                            if c == 2:
                                pe.wait_ge(v_ready, turn * 2 + (s + 1))
                                if not first:
                                    pe.wait_ge(y_out, turn * 2 + (s - 1))
                            if st >= 2:
                                outputs(turn, st - 2, turn * STEPS + (st - 1))
                            else:
                                outputs(turn - 1, st - 2 + STEPS, turn * STEPS + (st - 1))

                turns(pe, body)
                end = TURNS * STEPS
                pe.wait_ge(mix_out, end - 1)
                pe.wait_ge(cross_out, end - 1)
                products(STEPS - 1, end)
                outputs(TURNS - 1, STEPS - 2, end - 1)
                outputs(TURNS - 1, STEPS - 1, end)

            @block.scalar
            def _(act):
                def cross_copy(st, count):
                    act.wait_ge(cb_done, count)
                    for q in range(BPC):
                        last = nc.scalar.activation(cross[:, st % 2, q, :], pcb[q][:, 1, :], ACT.Copy)
                    last.then_inc(cross_out, 1)

                def body(turn, first):
                    for st in range(STEPS):
                        n = turn * STEPS + st
                        act.wait_ge(b_done, n + 1)
                        if not (first and st < 2):
                            act.wait_ge(cb_done, turn * STEPS + (st - 1))
                        nc.scalar.activation(bT[:, st % 2, :], pbT[:], ACT.Copy).then_inc(b_out, 1)
                        act.wait_ge(dec_masked, n + 1)
                        if not (first and st < 2):
                            act.wait_ge(mix_out, turn * STEPS + (st - 1))
                        for q in range(TPC):
                            cols = slice(q * P, (q + 1) * P)
                            last = nc.scalar.activation(
                                decay[:, st % 2, cols], masked[:, st % 2, cols], ACT.Exp,
                                bias=negcum[:, st % NCH * TPC + q, bass.ds(turn * 2 + st // NCH, 1)])
                        last.then_inc(dec_out, 1)
                        if not (first and st == 0):
                            if not (first and st < 3):
                                act.wait_ge(y_done, turn * STEPS + (st - 2))
                            cross_copy((st - 1) % STEPS, turn * STEPS + st)

                turns(act, body)
                act.wait_ge(y_done, TURNS * STEPS - 2)
                cross_copy(STEPS - 1, TURNS * STEPS)

            @block.vector
            def _(dve):
                def mix(st, count):
                    dve.wait_ge(cross_out, count)
                    dve.wait_ge(dec_out, count)
                    for q in range(BPC):
                        last = nc.vector.tensor_tensor(
                            mixT[:, st % 2, 2 * q:2 * q + 2, :], pcb[q][:, 0:3:2, :],
                            decay[:, st % 2, q * S:(q + 1) * S].rearrange("p (n l) -> p n l", l=P), ALU.mult)
                    last.then_inc(mix_out, 1)

                def take(turn, s, heads):
                    dve.wait_ge(y_done, heads * NCH)
                    dve.wait_ge(v_ready, heads)
                    cols = head_cols(turn, s)
                    head = bass.ds(turn * 2 + s, 1)
                    nc.vector.tensor_tensor(late[:], py[s][:, NT:, :], ecum[:, 1:NT:2, head]
                                            .broadcast_to([P, B, SHD]), ALU.mult)
                    nc.vector.tensor_tensor(val[:, :, cols], py[s][:, 0:NT, :], vskip[:, s, :, :],
                                            ALU.add).then_inc(late_out, 1)
                    dve.wait_ge(late_out, heads)
                    nc.vector.tensor_tensor(val[:, 1:NT:2, cols], val[:, 1:NT:2, cols], late[:],
                                            ALU.add).then_inc(y_out, 1)

                def body(turn, first):
                    for st in range(STEPS):
                        s, c = st // NCH, st % NCH
                        dve.wait_ge(dec_done, turn * STEPS + (st + 1))
                        if not (first and st < 2):
                            dve.wait_ge(dec_out, turn * STEPS + (st - 1))
                        nc.vector.tensor_tensor(masked[:, st % 2, :], pdec[:], mask[:], ALU.add).then_inc(dec_masked, 1)
                        dve.wait_ge(c_done, turn * STEPS + (st + 1))
                        if not (first and st < 2):
                            dve.wait_ge(cb_done, turn * STEPS + (st - 1))
                        nc.vector.tensor_copy(cT[:, st % 2, :], pcT[:]).then_inc(c_out, 1)
                        if not (first and st == 0):
                            if not (first and st < 3):
                                dve.wait_ge(y_done, turn * STEPS + (st - 2))
                            mix((st - 1) % STEPS, turn * STEPS + st)
                        if c == 2 and not (first and s == 0):
                            if s == 1:
                                take(turn, 0, turn * 2 + 1)
                            else:
                                take(turn - 1, 1, turn * 2)

                turns(dve, body)
                end = TURNS * STEPS
                dve.wait_ge(y_done, end - 2)
                mix(STEPS - 1, end)
                take(TURNS - 1, 1, SH)


def stage_ssm_out(chip, t, y, ident, ins):
    nc = chip.nc
    val, gateT = t["val"], t["gateT"]
    with ExitStack() as ctx:
        sb, pb = chip.memory(ctx)
        wout = sb("wout", [P, NC, D])
        staged = sb("staged", [P, 2, 2, DI])
        zT = sb("zT", [P, 2, NC, S])
        pt = [pb(f"pt{n}", [P, 2, S]) for n in range(4)]
        po = [pb(f"po{n}", [P, 2, D]) for n in range(2)]
        loaded, stage_done, turned = chip.sem("loaded"), chip.sem("stage_done"), chip.sem("turned")
        gated, projected, y_out = chip.sem("gated"), chip.sem("projected"), chip.sem("y_out")
        with nc.Block() as block:
            @block.sync
            def _(sp):
                sp.dma_start(wout[:], ins["w_out"]).then_inc(loaded, 16)

            @block.gpsimd
            def _(pool):
                def body(i):
                    after(pool, turned, i * 2)
                    for s in range(2):
                        nc.gpsimd.tensor_copy(staged[:, s, :, :],
                                              val[:, bass.ds(i * 4 + 2 * s, 2), :]).then_inc(stage_done, 1)

                repeat(pool, B // 2, body)

            @block.tensor
            def _(pe):
                pe.wait_ge(loaded, 16)
                def body(i):
                    for s in range(2):
                        pe.wait_ge(stage_done, i * 2 + (s + 1))
                        after(pe, gated, i * 2)
                        for blk in range(NC):
                            for n in range(2):
                                last = nc.tensor.transpose(pt[2 * s + blk // 2][:, blk % 2, n * P:(n + 1) * P],
                                                           staged[:, s, n, blk * P:(blk + 1) * P], ident[:])
                        last.then_inc(turned, 1)
                    for s in range(2):
                        pe.wait_ge(gated, i * 2 + (s + 1))
                        after(pe, y_out, i * 2)
                        for n in range(2):
                            for blk in range(NC):
                                last = nc.tensor.matmul(po[s][:, n, :], zT[:, s, blk, n * P:(n + 1) * P],
                                                        wout[:, blk, :], start=(blk == 0), stop=(blk == NC - 1))
                        last.then_inc(projected, 1)

                repeat(pe, B // 2, body)

            @block.scalar
            def _(act):
                def body(i):
                    for s in range(2):
                        act.wait_ge(projected, i * 2 + (s + 1))
                        nc.scalar.activation(y[:, bass.ds(i * 4 + 2 * s, 2), :], po[s][:],
                                             ACT.Copy).then_inc(y_out, 1)

                repeat(act, B // 2, body)

            @block.vector
            def _(dve):
                def body(i):
                    for s in range(2):
                        dve.wait_ge(turned, i * 2 + (s + 1))
                        after(dve, projected, i * 2)
                        for half in range(2):
                            blks = slice(2 * half, 2 * half + 2)
                            last = nc.vector.tensor_tensor(zT[:, s, blks, :], pt[2 * s + half][:],
                                                           gateT[:, blks, bass.ds(i * (2 * S) + s * S, S)], ALU.mult)
                        last.then_inc(gated, 1)

                repeat(dve, B // 2, body)



def stage_ffn(chip, xh, y, ins):
    nc = chip.nc
    WCOL = 2 * D
    with ExitStack() as ctx:
        sb, pb = chip.memory(ctx)
        wraw = sb("wraw", [P, NFH, WCOL])
        wh = sb("wh", [P, NFH, WCOL], F32R)
        wl = sb("wl", [P, NFH, WCOL], F32R)
        bias0 = sb("bias0", [P, NFH])
        bias1 = sb("bias1", [P, D])
        act16 = sb("act16", [P, 2, CHUNK], F16)
        hid = sb("hid", [P, 2, CHUNK], F32R)
        y16 = sb("y16", [P, TPC, D], F16)
        ph = [pb(f"ph{n}", [P, CHUNK]) for n in range(2)]
        acc = [pb(f"acc{n}", [P, D]) for n in range(TPC)]
        raw_loaded = chip.sem("raw_loaded")
        loaded, split_half, split_done = chip.sem("loaded"), chip.sem("split_half"), chip.sem("split_done")
        up_done, gelu_done, hid_done = chip.sem("up_done"), chip.sem("gelu_done"), chip.sem("hid_done")
        down_done, y_half, y_out = chip.sem("down_done"), chip.sem("y_half"), chip.sem("y_out")
        with nc.Block() as block:
            @block.sync
            def _(sp):
                sp.dma_start(wraw[:], ins["ffn_w"]).then_inc(raw_loaded, 16)
                sp.dma_start(bias0[:], ins["ffn_b0"]).then_inc(loaded, 16)
                sp.dma_start(bias1[:], ins["ffn_b1"]).then_inc(loaded, 16)

            @block.tensor
            def _(pe):
                pe.wait_ge(split_done, 2)

                def up(c, n):
                    parts = [(w, k) for k in range(KD) for w in (wh, wl)]
                    for m, (w, k) in enumerate(parts):
                        last = nc.tensor.matmul(ph[n % 2][:], w[:, n, k * P:(k + 1) * P],
                                                xh[:, k, bass.ts(c, CHUNK)], start=(m == 0), stop=(m == len(parts) - 1))
                    last.then_inc(up_done, 1)

                def down(n):
                    for t in range(TPC):
                        for m, w in enumerate((wh, wl)):
                            last = nc.tensor.matmul(acc[t][:], hid[:, n % 2, t * P:(t + 1) * P], w[:, n, D:2 * D],
                                                    start=(n == 0 and m == 0), stop=(n == NFH - 1 and m == 1))
                    last.then_inc(down_done, 1)

                def body(c):
                    for n in range(NFH + 1):
                        if n < NFH:
                            after(pe, gelu_done, c * NFH + max(n - 1, 0))
                            up(c, n)
                        if n == 1:
                            after(pe, y_half, c)
                        if n >= 1:
                            pe.wait_ge(hid_done, c * NFH + n)
                            down(n - 1)

                repeat(pe, NCH, body)

            @block.scalar
            def _(act):
                act.wait_ge(loaded, 32)
                def body(c):
                    for n in range(NFH):
                        act.wait_ge(up_done, c * NFH + (n + 1))
                        after(act, hid_done, c * NFH + max(n - 1, 0))
                        nc.scalar.activation(act16[:, n % 2, :], ph[n % 2][:], ACT.Gelu,
                                             bias=bias0[:, n:n + 1]).then_inc(gelu_done, 1)

                repeat(act, NCH, body)

            @block.vector
            def _(dve):
                dve.wait_ge(raw_loaded, 16)
                nc.vector.tensor_copy(flat(wh[:]), flat(wraw[:])).then_inc(split_half, 1)
                dve.wait_ge(split_half, 1)
                nc.vector.tensor_tensor(flat(wl[:]), flat(wraw[:]), flat(wh[:]).bitcast(F32),
                                        ALU.subtract).then_inc(split_done, 2)
                dve.wait_ge(loaded, 32)
                def body(c):
                    for n in range(NFH):
                        dve.wait_ge(gelu_done, c * NFH + (n + 1))
                        after(dve, down_done, c * NFH + max(n - 1, 0))
                        nc.vector.tensor_copy(hid[:, n % 2, :], act16[:, n % 2, :]).then_inc(hid_done, 1)
                    dve.wait_ge(down_done, c * NFH + NFH)
                    for t in range(TPC):
                        last = nc.vector.tensor_tensor(y16[:, t, :], acc[t][:], bias1[:], ALU.add)
                    last.then_inc(y_half, 1)
                    dve.wait_ge(y_half, c + 1)
                    nc.vector.tensor_copy(y[:, bass.ts(c, TPC), :], y16[:]).then_inc(y_out, 1)

                repeat(dve, NCH, body)


def program(nc, io):
    with ExitStack() as sems, ExitStack() as mem:
        chip = Chip(nc, sems)
        x = mem.enter_context(nc.sbuf_tensor("x", [P, NT, D], F32))
        y = mem.enter_context(nc.sbuf_tensor("y", [P, NT, D], F32))
        xh = mem.enter_context(nc.sbuf_tensor("xh", [P, KD, TOK], F32R))
        xl = mem.enter_context(nc.sbuf_tensor("xl", [P, KD, TOK], F32R))
        ident = mem.enter_context(nc.sbuf_tensor("ident", [P, P], F32))
        x_loaded = chip.sem("x_loaded")
        with nc.Block() as block:
            @block.sync
            def _(sp):
                sp.dma_start(x[:], io["x"]).then_inc(x_loaded, 16)
                sp.dma_start(ident[:], io["ident"]).then_inc(x_loaded, 16)
                sp.wait_ge(x_loaded, 32)
        stage_norm(chip, x, y, xh, xl, ident, False, True)
        with ExitStack() as att:
            sb, _ = chip.memory(att)
            vparts = sb("vparts", [P, NT, NH, VCOL], BF16)
            qk_dram = nc.dram_tensor("qk_parts", (2, KD, P, PARTS, TOK), BF16).ap()
            stage_qkv(chip, xh, xl, vparts, qk_dram, io)
            stage_attention(chip, vparts, qk_dram, y, ident, io)
        stage_norm(chip, x, y, xh, xl, ident, True, True)
        stage_moe(chip, xh, xl, y, ident, io)
        stage_norm(chip, x, y, xh, xl, ident, True, True)
        stage_ssm(chip, xh, xl, y, ident, io)
        stage_norm(chip, x, y, xh, xl, ident, True, True, half=True)
        stage_ffn(chip, xh, y, io)
        stage_norm(chip, x, y, xh, xl, ident, True, False, out=io["out"])



def slopes(n):
    start = 2.0 ** (-8.0 / n)
    return [start ** (i + 1) for i in range(n)]


def layouts(a):
    import numpy as np

    def bcast(v):
        return np.broadcast_to(v.reshape(1, -1), (P, v.size)).copy()

    out = {}
    out["x"] = a["L0_attn_hidden_states"].reshape(NT, P, D).transpose(1, 0, 2)
    w, bias = a["L0_attn_w_qkv"], a["L0_attn_b_qkv"]
    out["wqkv"] = w.reshape(KD, P, 3 * D).transpose(1, 0, 2)
    out["bqk"] = bias[:2 * D].reshape(2 * KD, P).T
    out["bv"] = bcast(bias[2 * D:])
    out["wproj"] = a["L0_attn_w_proj"].reshape(KD, P, D).transpose(1, 0, 2)
    out["bproj"] = bcast(a["L0_attn_b_proj"])
    alibi = np.zeros((PARTS, 2, NH, S), np.dtype("bfloat16"))
    left = np.array(slopes(NH), np.float32)
    for part in range(PARTS):
        alibi[part, 0] = left.astype(alibi.dtype)[:, None]
        left = left - left.astype(alibi.dtype).astype(np.float32)
        alibi[part, 1] = np.arange(S)
    out["alibi"] = alibi
    low = np.tril(np.ones((P, P), bool))
    out["ident"] = np.eye(P, dtype=np.float32)
    out["identb"] = np.eye(P).astype(np.dtype("bfloat16"))
    out["causal_add"] = np.where(low, 0.0, -BIG).astype(np.dtype("bfloat16"))

    out["router_w"] = a["L0_ffn_router_w"].reshape(KD, P, NE).transpose(1, 0, 2)
    out["router_b"] = bcast(a["L0_ffn_router_bias"])
    select = np.zeros((ROUTED + SHARED, 2, NE, P // FE, FE), np.float32)
    for j in range(ROUTED):
        for n in range(P // FE):
            select[j, :, j * (P // FE) + n, n, :] = 1.0
    cols = []
    for routed, shared in (("wg", "swg"), ("wu", "swu")):
        r = a["L0_ffn_" + routed].reshape(ROUTED, P // FE, KD, P, FE).transpose(0, 3, 2, 1, 4)
        sh = a["L0_ffn_" + shared].reshape(2, KD, P, SHARED // 2, P).transpose(0, 3, 2, 1, 4)
        cols.append(np.concatenate([r.reshape(ROUTED, P, D), sh.reshape(SHARED, P, D)]))
    cols.append(np.concatenate([a["L0_ffn_wd"].reshape(ROUTED, P, D), a["L0_ffn_swd"].reshape(SHARED, P, D)]))
    cols.append(select.reshape(ROUTED + SHARED, P, P))
    out["experts"] = np.concatenate(cols, axis=2)
    w_in = a["L1_attn_W_in"].T
    nbc = SH * SN
    edge = np.zeros((D, CB_IN * P), np.float32)
    edge[:, :2 * DI] = w_in[:, :2 * DI]
    edge[:, 2 * DI:2 * DI + SH] = w_in[:, 2 * DI + 2 * nbc:]
    out["w_in"] = edge.reshape(KD, P, CB_IN * P).transpose(1, 0, 2)
    bc = w_in[:, 2 * DI:2 * DI + 2 * nbc].reshape(KD, P, 2, SH, SN)
    out["w_bc"] = bc.transpose(3, 1, 2, 0, 4).reshape(SH, P, 2 * KD * P)
    chan = np.concatenate([a["L1_attn_conv_w"].reshape(DI, TAPS), a["L1_attn_conv_b"].reshape(DI, 1)], axis=1)
    out["chan"] = chan.reshape(NC, P, TAPS + 1).transpose(1, 0, 2)
    out["head"] = np.stack([a["L1_attn_dt_bias"], a["L1_attn_A_log"]], axis=1)
    out["tri"] = np.stack([low.T, low & ~np.eye(P, dtype=bool)], axis=1).astype(np.float32)
    rows = np.zeros((PARTS, SH, SH, P), np.float32)
    for h in range(SH):
        rows[:, h, h] = 1.0
    out["head_rows"] = rows.reshape(PARTS * SH, SH * P).astype(np.dtype("bfloat16"))
    out["mask_turned"] = np.tile(np.where(low.T, 0.0, -BIG), (1, TPC)).astype(np.float32)
    out["skip"] = bcast(a["L1_attn_D_param"])
    out["w_out"] = a["L1_attn_W_out"].T.reshape(NC, P, D).transpose(1, 0, 2)

    w0 = a["L1_ffn_W0"].T.reshape(KD, P, NFH, P).transpose(1, 2, 0, 3).reshape(P, NFH, D)
    w1 = a["L1_ffn_W1"].T.reshape(NFH, P, D).transpose(1, 0, 2)
    out["ffn_w"] = np.concatenate([w0, w1], axis=2)
    out["ffn_b0"] = a["L1_ffn_bias0"].reshape(NFH, P).T
    out["ffn_b1"] = bcast(a["L1_ffn_bias1"])
    return {k: np.ascontiguousarray(v) for k, v in out.items()}


def kernel(**inputs):
    import concourse.bacc as bacc
    import numpy as np
    from concourse.bass_utils import run_bass_kernel_spmd

    arrays = layouts({k: np.asarray(v) for k, v in inputs.items()})
    nc = bacc.Bacc("TRN2", target_bir_lowering=False, num_devices=1)
    io = {}
    for name, v in arrays.items():
        io[name] = nc.dram_tensor(f"in_{name}", v.shape, mybir.dt.from_np(v.dtype), kind="ExternalInput").ap()
    io["out"] = nc.dram_tensor("result", (P, NT, D), mybir.dt.from_np(np.dtype("float32")),
                               kind="ExternalOutput").ap()
    program(nc, io)
    r = run_bass_kernel_spmd(nc, [{f"in_{k}": v for k, v in arrays.items()}], core_ids=[0])
    got = np.asarray(r.results[0]["result"])
    return got.reshape(P, NT, D).transpose(1, 0, 2).reshape(B, S, D)
```
